# Optimizing a Trainium2 kernel written in Bass

```python
import numpy as np
import jax
import jax.numpy as jnp

def _softmax(x, axis=-1):
    return jax.nn.softmax(x, axis=axis)

def _gelu(x):
    return jax.nn.gelu(x, approximate=True)

def _silu(x):
    return jax.nn.silu(x)

def _sigmoid(x):
    return jax.nn.sigmoid(x)

def _layernorm(x, axis=-1, eps=1e-05):
    m = jnp.mean(x, axis=axis, keepdims=True)
    v = jnp.var(x, axis=axis, keepdims=True)
    return (x - m) / jnp.sqrt(v + eps)

def _scatter_add(tgt, idx, src, axis=0):
    return tgt.at[idx].add(src)

def _segment_sum(src, seg, n):
    return jax.ops.segment_sum(src, seg, n)
kernel_name = 'mk_seq_preln_d1_jaxref_r4_27dd41'

def setup_inputs(seed: int=0):
    np.random.seed(seed)
    _w = jnp.asarray

    def _L0_attn_setup():
        import jax, jax.numpy as jnp
        import numpy as np
        D_MODEL = 256
        N_HEADS = 16
        D_K = D_MODEL // N_HEADS
        THETA = 10000.0
        BATCH = 1
        SEQ = 1024

        def _rope(x, pos, inv_freq):
            angles = pos[:, None].astype(jnp.float32) * inv_freq
            cos = jnp.repeat(jnp.cos(angles), 2, axis=-1)
            sin = jnp.repeat(jnp.sin(angles), 2, axis=-1)
            x_rot = jnp.stack([-x[..., 1::2], x[..., 0::2]], axis=-1).reshape(x.shape)
            return x * cos + x_rot * sin
        key = jax.random.key(seed)
        ks = jax.random.split(key, 5)
        std = (2.0 / (D_MODEL + D_MODEL)) ** 0.5
        mk = lambda k: jax.random.truncated_normal(k, -3.0, 3.0, (D_MODEL, D_MODEL), jnp.float32) * std
        return {'x': jax.random.normal(ks[0], (BATCH, SEQ, D_MODEL), jnp.float32), 'Wq': mk(ks[1]), 'Wk': mk(ks[2]), 'Wv': mk(ks[3]), 'Wo': mk(ks[4])}
    _L0_attn_in = _L0_attn_setup()

    def _L0_ffn_setup():
        import jax, jax.numpy as jnp
        import numpy as np
        DIM = 256
        HIDDEN = 768
        SCALE = 1.0 / 127.0

        def _dequant(w_int, dtype):
            return w_int.astype(dtype) * jnp.asarray(SCALE, dtype)
        key = jax.random.key(seed)
        k_x, k_g, k_u, k_d = jax.random.split(key, 4)
        x = jax.random.normal(k_x, (4, 512, DIM), dtype=jnp.float32)
        w_gate = jax.random.randint(k_g, (HIDDEN, DIM), -127, 128, dtype=jnp.int32)
        w_up = jax.random.randint(k_u, (HIDDEN, DIM), -127, 128, dtype=jnp.int32)
        w_down = jax.random.randint(k_d, (DIM, HIDDEN), -127, 128, dtype=jnp.int32)
        return {'x': x, 'w_gate': w_gate, 'w_up': w_up, 'w_down': w_down}
    _L0_ffn_in = _L0_ffn_setup()
    _d = {'L0_attn_x': _L0_attn_in['x'], 'L0_attn_Wq': _L0_attn_in['Wq'], 'L0_attn_Wk': _L0_attn_in['Wk'], 'L0_attn_Wv': _L0_attn_in['Wv'], 'L0_attn_Wo': _L0_attn_in['Wo'], 'L0_ffn_w_gate': _L0_ffn_in['w_gate'], 'L0_ffn_w_up': _L0_ffn_in['w_up'], 'L0_ffn_w_down': _L0_ffn_in['w_down']}
    _x0 = _d['L0_attn_x']
    _d['L0_attn_x'] = jax.random.normal(jax.random.fold_in(jax.random.key(seed), 1), (8, 512, 256), dtype=_x0.dtype)
    del _x0
    return _d

def reference(L0_attn_x, L0_attn_Wq, L0_attn_Wk, L0_attn_Wv, L0_attn_Wo, L0_ffn_w_gate, L0_ffn_w_up, L0_ffn_w_down):

    def _L0_attn_ref(x, Wq, Wk, Wv, Wo):
        import jax, jax.numpy as jnp
        import numpy as np
        D_MODEL = 256
        N_HEADS = 16
        D_K = D_MODEL // N_HEADS
        THETA = 10000.0
        BATCH = 1
        SEQ = 1024

        def _rope(x, pos, inv_freq):
            angles = pos[:, None].astype(jnp.float32) * inv_freq
            cos = jnp.repeat(jnp.cos(angles), 2, axis=-1)
            sin = jnp.repeat(jnp.sin(angles), 2, axis=-1)
            x_rot = jnp.stack([-x[..., 1::2], x[..., 0::2]], axis=-1).reshape(x.shape)
            return x * cos + x_rot * sin
        b, s, _ = x.shape
        h, dk = (N_HEADS, D_K)
        proj = lambda W: jnp.einsum('bsi,oi->bso', x, W).reshape(b, s, h, dk).transpose(0, 2, 1, 3)
        q = proj(Wq)
        k = proj(Wk)
        v = proj(Wv)
        pos = jnp.arange(s)
        inv_freq = 1.0 / THETA ** (jnp.arange(0, dk, 2, dtype=jnp.float32) / dk)
        q = _rope(q, pos, inv_freq)
        k = _rope(k, pos, inv_freq)
        scores = jnp.einsum('bhqd,bhkd->bhqk', q, k) / jnp.sqrt(jnp.asarray(dk, jnp.float32))
        causal_mask = jnp.arange(s)[None, :] > jnp.arange(s)[:, None]
        scores = jnp.where(causal_mask, -jnp.inf, scores)
        weights = jax.nn.softmax(scores, axis=-1)
        out = jnp.einsum('bhqk,bhkd->bhqd', weights, v)
        out = out.transpose(0, 2, 1, 3).reshape(b, s, h * dk)
        return jnp.einsum('bsi,oi->bso', out, Wo)

    def _L0_ffn_ref(x, w_gate, w_up, w_down):
        import jax, jax.numpy as jnp
        import numpy as np
        DIM = 256
        HIDDEN = 768
        SCALE = 1.0 / 127.0

        def _dequant(w_int, dtype):
            return w_int.astype(dtype) * jnp.asarray(SCALE, dtype)
        wg = _dequant(w_gate, x.dtype)
        wu = _dequant(w_up, x.dtype)
        wd = _dequant(w_down, x.dtype)
        gate = jnp.einsum('bsd,hd->bsh', x, wg)
        up = jnp.einsum('bsd,hd->bsh', x, wu)
        h = jax.nn.silu(gate) * up
        return jnp.einsum('bsh,dh->bsd', h, wd)
    x = L0_attn_x
    x = x + _L0_attn_ref(_layernorm(x, axis=-1), L0_attn_Wq, L0_attn_Wk, L0_attn_Wv, L0_attn_Wo)
    x = x + _L0_ffn_ref(_layernorm(x, axis=-1), L0_ffn_w_gate, L0_ffn_w_up, L0_ffn_w_down)
    return x

_drawn_inputs = setup_inputs


def setup_inputs(seed=0):
    import zlib

    import numpy as np

    out = dict(_drawn_inputs(seed))
    spreads = {}
    factors = {}
    for name, (base, spread) in spreads.items():
        noise = np.random.default_rng([zlib.crc32(name.encode()), seed]).standard_normal(out[name].shape)
        drawn = base * np.exp(spread * noise) if base else spread * noise
        out[name] = jnp.asarray(drawn.astype(out[name].dtype))
    for name, factor in factors.items():
        out[name] = (out[name] * factor).astype(out[name].dtype)
    return out
```

```python
from contextlib import ExitStack

import numpy as np

import concourse.bass as bass
from concourse import mybir

F32 = mybir.dt.float32
F32R = mybir.dt.float32r
BF16 = mybir.dt.bfloat16
I32 = mybir.dt.int32
ACT = mybir.ActivationFunctionType
ALU = mybir.AluOpType
AX = mybir.AxisListType

P = 128
NB = 8
S = 512
D = 256
H = 16
DK = D // H
HID = 768
TT = S // P
KT = D // P
FT = HID // P
G = 4
NG = H // G
UNITS = 10
TERMS_Q = (0, 0, 0, 1, 1, 2)
TERMS_K = (0, 1, 2, 0, 1, 0)
STACK = 16 * len(TERMS_Q)
MAXROWS = 2
EPS = 1e-5
DEQ = float(np.float32(1.0 / 127.0))
BELOW_ALL = -1e30
SLOTS = 6 * UNITS
GATES = ((0,), (1,), (2, 3), (4, 5))

S_USES = NG * UNITS + NG
T_USES = NG * UNITS + FT
T_LAST = {0: T_USES, 1: T_USES - 2, 2: T_USES - 1}
SWAP_PAIRS = [i ^ 1 for i in range(32)]


def wait_for(eng, sem, per, batch, shift, count):
    least = shift * per + count
    if isinstance(batch, int):
        if batch * per + least > 0:
            eng.wait_ge(sem, batch * per + least)
    else:
        assert per + least > 0
        eng.wait_ge(sem, batch * per + least)


def max_use(g, u):
    return UNITS * g + u + (g if u > 2 else max(g - 1, 0))


def turn_use(g):
    return UNITS * (g + 1) + 3 + g if g < NG - 1 else S_USES - 1


def preln_block(nc, x, wqkv, wo, wg, wu, wd, cos_t, sin_t, out):
    with ExitStack() as ctx:
        def sb(name, shape, dt):
            return ctx.enter_context(nc.sbuf_tensor(name, shape, dt))

        def pb(name, shape, dt):
            return ctx.enter_context(nc.psum_tensor(name, shape, dt))

        def sem(name):
            return ctx.enter_context(nc.semaphore(name))

        qs = sb("q_stack", [P, H, S], BF16)
        ks = sb("k_stack", [P, H, S], BF16)
        prob = sb("prob", [P, UNITS, S], F32)
        wqkv_hi, wqkv_lo = sb("wqkv_hi", [P, KT, 3 * D], F32R), sb("wqkv_lo", [P, KT, 3 * D], F32R)
        wo_hi, wo_lo = sb("wo_hi", [P, KT, D], F32R), sb("wo_lo", [P, KT, D], F32R)
        wg_hi, wg_lo = sb("wg_hi", [P, KT, HID], F32R), sb("wg_lo", [P, KT, HID], F32R)
        wu_hi, wu_lo = sb("wu_hi", [P, KT, HID], F32R), sb("wu_lo", [P, KT, HID], F32R)
        wd_hi, wd_lo = sb("wd_hi", [P, FT, D], F32R), sb("wd_lo", [P, FT, D], F32R)
        cos_sb, sin_sb = sb("cos_sb", [P, S], F32), sb("sin_sb", [P, S], F32)
        xt = sb("xt", [P, TT, D], F32)
        res = sb("res", [P, TT, D], F32)
        x1T_hi, x1T_lo = sb("x1T_hi", [P, KT, S], F32R), sb("x1T_lo", [P, KT, S], F32R)
        x2T_hi, x2T_lo = sb("x2T_hi", [P, KT, S], F32R), sb("x2T_lo", [P, KT, S], F32R)
        rope = sb("rope", [P, 2, 2, S], F32)
        part = sb("part", [P, 2, 3, S], BF16)
        vaug = sb("vaug", [P, TT, H, 32], F32)
        sil = sb("sil", [P, 2, S], F32)
        h_hi, h_lo = sb("h_hi", [P, FT, S], F32R), sb("h_lo", [P, FT, S], F32R)
        oT = sb("oT", [P, S], F32)
        rsum = sb("rsum", [P, TT, G, 1], F32)
        attn = sb("attn", [P, TT, H, DK], F32)
        aT_hi, aT_lo = sb("aT_hi", [P, KT, S], F32R), sb("aT_lo", [P, KT, S], F32R)
        nm = sb("neg_max", [P, NG, TT, G], F32)
        nmb = sb("neg_max_parts", [P, NG, TT, G, MAXROWS], BF16)
        mrow = sb("max_rows", [G * MAXROWS, 2, S], BF16)
        st1, mv1 = sb("st1", [P, TT, 6], F32), sb("mv1", [P, TT, 2], F32)
        st2, mv2 = sb("st2", [P, TT, 6], F32), sb("mv2", [P, TT, 2], F32)
        rs1, rs2 = sb("rs1", [P, 2, TT], F32), sb("rs2", [P, 2, TT], F32)
        minus_half = sb("minus_half", [P, TT], F32)
        ident, identb = sb("ident", [P, P], F32), sb("identb", [P, P], BF16)
        hide = sb("hide", [P, 2, P], BF16)

        smax = pb("smax", [P, 2, S], F32)
        sexp = pb("sexp", [P, 3, S], F32)
        pvo = pb("pvo", [P, S], F32)
        wk = pb("work", [P, 2, S], F32)
        smax_b = smax[:, :, :].bitcast(BF16)

        scr = nc.dram_tensor("parts", (4, 3, P, S), BF16, kind="Internal").ap()

        names = """w_in c_in x_in res_in out_sent parts_sent stack_in0 stack_in1
            m_in0 m_in1 m_in2 m_in3
            iden hidden ones_set half_set vones w_cast w_hi w_lo
            stat1 aggr1 var1 root1 norm1 stat2 aggr2 var2 root2 norm2
            x1T_full x1T_high x1T_low x2T_full x2T_high x2T_low
            qk_full qk_cos qk_swap qk_sin qk_rot qk_hi qk_rest qk_mid qk_low
            v_full v_out s_full s_out split_hi split t_full t_out masked
            pv_full o_copied o_turned o_inv o_norm aT_full aT_high aT_low wo_full wo_out
            up_full h_full h_high h_low y_full y_out""".split()
        E = {n: sem(n) for n in names}

        xv = x.rearrange("b (t p) d -> b p t d", p=P)
        ov = out.rearrange("b (t p) d -> b p t d", p=P)
        raw_f = rope[:, :, :, :].rearrange("p a b s -> p (a b s)")
        raw_i = prob[:, :, :].rearrange("p u s -> p (u s)")
        raw_qkv = raw_f[:, 0:KT * 3 * D].rearrange("p (k o) -> p k o", k=KT)
        raw_wo = raw_f[:, KT * 3 * D:KT * 4 * D].rearrange("p (k o) -> p k o", k=KT)

        def raw_ffn(n, k):
            return raw_i[:, n * KT * HID:(n + 1) * KT * HID].rearrange("p (k o) -> p k o", k=k)

        block = ctx.enter_context(nc.Block())

        def turns(eng, turn):
            turn(-1, False, False, True)
            turn(0, False, True, True)
            with eng.Fori(1, NB - 1) as b:
                turn(b, True, True, True)
            turn(NB - 1, True, True, False)
            turn(NB, True, False, False)

        @block.sync
        def _(sp):
            def max_rows(b, g):
                wait_for(sp, E["s_out"], S_USES, b, 0, turn_use(g) + 1)
                for j in range(G):
                    sp.dma_start(qs[STACK:STACK + MAXROWS, G * g + j, :],
                                 mrow[MAXROWS * j:MAXROWS * (j + 1), g % 2, :]).then_inc(E[f"m_in{g}"], 16)

            def store_parts(b, t):
                sp.dma_start(scr[t].rearrange("n r s -> r n s"), part[:, t % 2, :, :])\
                    .then_inc(E["parts_sent"], 16)

            def load_stack(b, t):
                dst, terms = ((qs, TERMS_Q), (ks, TERMS_K))[t % 2]
                for n, p in enumerate(terms):
                    sp.dma_start(dst[DK * n:DK * (n + 1), 8 * (t // 2):8 * (t // 2 + 1), :],
                                 scr[t, p].rearrange("(h d) s -> d h s", d=DK))\
                        .then_inc(E[f"stack_in{t // 2}"], 16)

            def turn(b, prev, cur, nxt):
                for q in range(SLOTS):
                    if nxt and q == 16:
                        if prev:
                            wait_for(sp, E["x2T_full"], KT, b, -1, KT)
                        else:
                            wait_for(sp, E["x1T_full"], KT, b, 0, KT)
                        sp.dma_start(xt[:, :, :], xv[b + 1]).then_inc(E["x_in"], 16)
                    if cur and q in (14, 24, 34, 44):
                        max_rows(b, q // 10 - 1)
                    if prev and q == 26:
                        wait_for(sp, E["y_out"], KT, b, -1, 2)
                        sp.dma_start(ov[b - 1], res[:, :, :]).then_inc(E["out_sent"], 16)
                    if cur and q == 30:
                        wait_for(sp, E["out_sent"], 16, b, -1, 16)
                        sp.dma_start(res[:, :, :], xv[b]).then_inc(E["res_in"], 16)
                    if nxt and q in (46, 49):
                        t = (q - 46) // 3
                        wait_for(sp, E["qk_low"], 4, b, 1, t + 1)
                        store_parts(b, t)
                        wait_for(sp, E["parts_sent"], 64, b, 1, 16 * (t + 1))
                        load_stack(b, t)
                    if nxt and q == 59:
                        wait_for(sp, E["qk_low"], 4, b, 1, 4)
                        store_parts(b, 2)
                        wait_for(sp, E["t_full"], T_USES, b, 0, NG * UNITS)
                        store_parts(b, 3)
                        wait_for(sp, E["parts_sent"], 64, b, 1, 64)
                        load_stack(b, 2)
                        load_stack(b, 3)

            sp.dma_start(raw_qkv, wqkv.rearrange("(k p) o -> p k o", p=P)).then_inc(E["w_in"], 16)
            sp.dma_start(raw_wo, wo.rearrange("(k p) o -> p k o", p=P)).then_inc(E["w_in"], 16)
            turns(sp, turn)
            wait_for(sp, E["out_sent"], 16, NB, 0, 0)

        @block.gpsimd
        def _(pool):
            pool.memset(ident[:, :], 0.0).then_inc(E["iden"], 1)
            pool.memset(hide[:, :, :], 0.0).then_inc(E["hidden"], 1)
            pool.memset(minus_half[:, :], -0.5).then_inc(E["half_set"], 1)
            pool.memset(vaug[:, :, :, DK:32], 1.0).then_inc(E["vones"], 1)
            pool.wait_ge(E["iden"], 1)
            pool.affine_select(out=ident[:, :], in_=ident[:, :], compare_op=ALU.not_equal, fill=1.0,
                               base=0, pattern=[[-1, P]], channel_multiplier=1).then_inc(E["iden"], 1)
            pool.wait_ge(E["hidden"], 1)
            pool.affine_select(out=hide[:, :, :], in_=hide[:, :, :], compare_op=ALU.is_ge,
                               fill=BELOW_ALL, base=0, pattern=[[0, 2], [-1, P]],
                               channel_multiplier=1).then_inc(E["hidden"], 1)

            def root(b, shift, rs, var, done):
                wait_for(pool, var, 1, b, shift, 1)
                pool.tensor_tensor(rs[:, 1, :], rs[:, 0, :], minus_half[:, :], ALU.pow).then_inc(done, 1)

            def keep(b, g, u):
                wait_for(pool, E["t_out"], T_USES, b, 0, UNITS * g + u + 1)
                if u % 5 == 2:
                    v = prob[:, u - 2:u + 1:2, 0:P]
                else:
                    v = prob[:, u, :].rearrange("p (k c) -> p k c", c=P)
                    v = v[:, 0:4:3, :] if u % 5 < 4 else v[:, 0:4:2, :]
                pool.affine_select(out=v, in_=v, compare_op=ALU.is_ge, fill=0.0, base=0,
                                   pattern=[[0, 2], [1, P]], channel_multiplier=-1).then_inc(E["masked"], 2)

            def rotate(b, t):
                wait_for(pool, E["qk_swap"], 8, b, 1, 2 * t + 2)
                pool.tensor_tensor(rope[:, t % 2, 1, :], rope[:, t % 2, 1, :], sin_sb[:, :], ALU.mult)\
                    .then_inc(E["qk_sin"], 1)
                wait_for(pool, E["qk_sin"], 4, b, 1, t + 1)
                pool.tensor_tensor(rope[:, t % 2, 0, :], rope[:, t % 2, 0, :], rope[:, t % 2, 1, :], ALU.add)\
                    .then_inc(E["qk_rot"], 1)

            def turn(b, prev, cur, nxt):
                for q in range(SLOTS):
                    if prev and q == 10:
                        root(b, -1, rs2, E["var2"], E["root2"])
                    if nxt and q == 26:
                        root(b, 1, rs1, E["var1"], E["root1"])
                    if cur and q >= 20:
                        g, u = (q - 20) // 10, q % 10
                        if u % 5:
                            keep(b, g, u)
                    if nxt and q in (42, 45, 48, 51):
                        rotate(b, (q - 42) // 3)

            turns(pool, turn)

        @block.scalar
        def _(act):
            act.dma_start(cos_sb[:, :], cos_t).then_inc(E["c_in"], 16)
            act.dma_start(sin_sb[:, :], sin_t).then_inc(E["c_in"], 16)
            act.dma_start(raw_ffn(0, KT).bitcast(I32), wg.rearrange("(k p) o -> p k o", p=P)).then_inc(E["w_in"], 16)
            act.dma_start(raw_ffn(1, KT).bitcast(I32), wu.rearrange("(k p) o -> p k o", p=P)).then_inc(E["w_in"], 16)
            act.dma_start(raw_ffn(2, FT).bitcast(I32), wd.rearrange("(k p) o -> p k o", p=P)).then_inc(E["w_in"], 16)
            act.wait_ge(E["w_in"], 80)
            act.activation(wqkv_hi[:, :, :], raw_qkv, ACT.Copy).then_inc(E["w_hi"], 1)
            act.activation(wo_hi[:, :, :], raw_wo, ACT.Copy).then_inc(E["w_hi"], 1)
            for n, (dst, k) in enumerate(((wg_hi, KT), (wu_hi, KT), (wd_hi, FT))):
                act.wait_ge(E["w_cast"], n + 1)
                act.activation(dst[:, :, :], raw_ffn(n, k), ACT.Copy).then_inc(E["w_hi"], 1)

            def high(b, shift, full, done, dst, k):
                wait_for(act, full, KT, b, shift, k + 1)
                act.activation(dst[:, k, :], wk[:, k, :], ACT.Copy).then_inc(done, 1)

            def values(b, i):
                wait_for(act, E["v_full"], 2, b, 0, i + 1)
                wait_for(act, E["pv_full"], NG, b, -1, NG)
                act.activation(vaug[:, 2 * i:2 * i + 2, :, 0:DK],
                               wk[:, i, :].rearrange("p (t h d) -> p t h d", t=2, d=DK), ACT.Copy)\
                    .then_inc(E["v_out"], 1)

            def exps(b, g, u):
                k = UNITS * g + u
                wait_for(act, E["t_full"], T_USES, b, 0, k + 1)
                if u == 0:
                    wait_for(act, E["pv_full"], NG, b, 0, g)
                act.activation(prob[:, u, :], sexp[:, k % 3, :], ACT.Exp, scale=DK ** -0.5)\
                    .then_inc(E["t_out"], 1)

            def silu(b, n):
                k = NG * UNITS + n
                wait_for(act, E["t_full"], T_USES, b, -1, k + 1)
                if n >= 2:
                    wait_for(act, E["h_low"], FT, b, -1, n - 1)
                act.activation(sil[:, n % 2, :], sexp[:, k % 3, :], ACT.Silu, scale=DEQ)\
                    .then_inc(E["t_out"], 1)

            def hidden_high(b, n):
                wait_for(act, E["h_full"], FT, b, -1, n + 1)
                act.activation(h_hi[:, n, :], sil[:, n % 2, :], ACT.Copy).then_inc(E["h_high"], 1)

            def copy_o(b, shift, g):
                wait_for(act, E["pv_full"], NG, b, shift, g + 1)
                wait_for(act, E["o_turned"], NG, b, shift, g)
                act.activation(oT[:, :], pvo[:, :], ACT.Copy).then_inc(E["o_copied"], 1)

            def turn(b, prev, cur, nxt):
                for q in range(SLOTS):
                    if prev and q == 1:
                        copy_o(b, -1, NG - 1)
                    if cur and q in (33, 43, 53):
                        copy_o(b, 0, q // 10 - 3)
                    if cur and q in (4, 5):
                        values(b, q - 4)
                    if prev and q in (6, 7):
                        high(b, -1, E["aT_full"], E["aT_high"], aT_hi, q - 6)
                    if prev and q in (15, 16):
                        high(b, -1, E["x2T_full"], E["x2T_high"], x2T_hi, q - 15)
                    if prev and 16 <= q < 20:
                        for n in GATES[q - 16]:
                            silu(b, n)
                            if n:
                                hidden_high(b, n - 1)
                    if prev and q == 20:
                        hidden_high(b, FT - 1)
                    if cur and q >= 20:
                        exps(b, (q - 20) // 10, q % 10)
                    if nxt and q in (37, 38):
                        high(b, 1, E["x1T_full"], E["x1T_high"], x1T_hi, q - 37)
                    if nxt and q in (43, 46, 49, 52):
                        t = (q - 43) // 3
                        wait_for(act, E["qk_rot"], 4, b, 1, t + 1)
                        wait_for(act, E["parts_sent"], 64, b, 1, 16 * (t - 1))
                        act.activation(part[:, t % 2, 0, :], rope[:, t % 2, 0, :], ACT.Copy)\
                            .then_inc(E["qk_hi"], 1)
                    if nxt and q in (44, 47, 50, 53):
                        t = (q - 44) // 3
                        wait_for(act, E["qk_rest"], 4, b, 1, t + 1)
                        act.activation(part[:, t % 2, 1, :], rope[:, t % 2, 0, :], ACT.Copy)\
                            .then_inc(E["qk_mid"], 1)

            turns(act, turn)

        @block.vector
        def _(dve):
            dve.memset(ks[STACK:STACK + MAXROWS, :, :], 1.0).then_inc(E["ones_set"], 1)
            dve.wait_ge(E["w_in"], 80)
            for n, k in enumerate((KT, KT, FT)):
                dve.tensor_copy(raw_ffn(n, k), raw_ffn(n, k).bitcast(I32)).then_inc(E["w_cast"], 1)
            for n, (dst, src, hi) in enumerate(((wqkv_lo[:, :, :], raw_qkv, wqkv_hi[:, :, :]),
                                                (wo_lo[:, :, :], raw_wo, wo_hi[:, :, :]),
                                                (wg_lo[:, :, :], raw_ffn(0, KT), wg_hi[:, :, :]),
                                                (wu_lo[:, :, :], raw_ffn(1, KT), wu_hi[:, :, :]),
                                                (wd_lo[:, :, :], raw_ffn(2, FT), wd_hi[:, :, :]))):
                if n >= 2:
                    dve.wait_ge(E["w_cast"], n - 1)
                dve.wait_ge(E["w_hi"], n + 1)
                dve.tensor_tensor(dst, src, hi, ALU.subtract).then_inc(E["w_lo"], 1)
            dve.wait_ge(E["iden"], 2)
            dve.tensor_copy(identb[:, :], ident[:, :]).then_inc(E["iden"], 1)

            def norm_stats(b, shift, src, st, mv, rs, which):
                for i in range(TT):
                    last = dve.bn_stats(st[:, i, :], src[:, i, :])
                last.then_inc(E["stat" + which], 1)
                wait_for(dve, E["stat" + which], 1, b, shift, 1)
                for i in range(TT):
                    dve.bn_aggr(mv[:, i, :], st[:, i, :]).then_inc(E["aggr" + which], 2)
                wait_for(dve, E["aggr" + which], 2 * TT, b, shift, 2 * TT)
                dve.tensor_scalar(rs[:, 0, :], mv[:, :, 1], EPS, None, ALU.add).then_inc(E["var" + which], 1)

            def norm_apply(b, shift, dst, src, mv, rs, which):
                wait_for(dve, E["root" + which], 1, b, shift, 1)
                for i in range(TT):
                    last = dve.tensor_scalar(dst[:, i, :], src[:, i, :], mv[:, i, 0:1], rs[:, 1, i:i + 1],
                                             ALU.subtract, ALU.mult)
                last.then_inc(E["norm" + which], 1)

            def low(b, shift, high, done, dst, hi, k):
                wait_for(dve, high, KT, b, shift, k + 1)
                dve.tensor_tensor(dst[:, k, :], wk[:, k, :], hi[:, k, :], ALU.subtract).then_inc(done, 1)

            def row_max(b, g, u):
                use, r, v = max_use(g, u), u // 5, u % 5
                bank = smax[:, use % 2, :]
                wait_for(dve, E["s_full"], S_USES, b, 0, use + 1)
                if v == 4:
                    last = dve.tensor_reduce(nm[:, g, 1, 2 * r:2 * r + 2],
                                             bank.rearrange("p (h c) -> p h c", h=2), AX.X, ALU.max, negate=True)
                else:
                    h = 2 * r + v // 2
                    if v % 2 == 0:
                        last = dve.tensor_reduce(nm[:, g, 3, h:h + 1], bank, AX.X, ALU.max, negate=True)
                    else:
                        dve.tensor_reduce(nm[:, g, 2, h:h + 1], bank[:, 0:3 * P], AX.X, ALU.max, negate=True)
                        last = dve.tensor_reduce(nm[:, g, 0, h:h + 1], bank[:, 3 * P:S], AX.X, ALU.max, negate=True)
                last.then_inc(E["s_out"], 1)

            def split_max(b, g):
                wait_for(dve, E["s_out"], S_USES, b, 0, max_use(g, UNITS - 1) + 1)
                dve.tensor_copy(nmb[:, g, :, :, 0], nm[:, g, :, :]).then_inc(E["split_hi"], 1)
                wait_for(dve, E["split_hi"], NG, b, 0, g + 1)
                dve.tensor_tensor(nmb[:, g, :, :, 1], nm[:, g, :, :], nmb[:, g, :, :, 0], ALU.subtract)\
                    .then_inc(E["split"], 1)

            def copy_max(b, g):
                use = turn_use(g)
                wait_for(dve, E["s_full"], S_USES, b, 0, use + 1)
                if g < 2:
                    wait_for(dve, E[f"m_in{g + 2}"], 64, b, -1, 64)
                else:
                    wait_for(dve, E[f"m_in{g - 2}"], 64, b, 0, 64)
                dve.tensor_copy(mrow[:, g % 2, :], smax_b[0:G * MAXROWS, use % 2, 0:S])\
                    .then_inc(E["s_out"], 1)

            def attn_norm(b, shift, g):
                o = pvo[:, :].rearrange("p (t h c) -> p t h c", t=TT, h=G)
                wait_for(dve, E["o_turned"], NG, b, shift, g + 1)
                dve.reciprocal(rsum[:, :, :, :], o[:, :, :, DK:DK + 1]).then_inc(E["o_inv"], 1)
                wait_for(dve, E["o_inv"], NG, b, shift, g + 1)
                if g == 0:
                    wait_for(dve, E["aT_full"], KT, b, shift - 1, KT)
                dve.tensor_tensor(attn[:, :, G * g:G * (g + 1), :], o[:, :, :, 0:DK],
                                  rsum[:, :, :, :].broadcast_to([P, TT, G, DK]), ALU.mult)\
                    .then_inc(E["o_norm"], 1)

            def hidden_full(b, n):
                wait_for(dve, E["up_full"], FT, b, -1, n + 1)
                wait_for(dve, E["t_out"], T_USES, b, -1, NG * UNITS + n + 1)
                dve.scalar_tensor_tensor(out=sil[:, n % 2, :], in0=wk[:, n % 2, :], scalar=DEQ,
                                         in1=sil[:, n % 2, :], op0=ALU.mult, op1=ALU.mult)\
                    .then_inc(E["h_full"], 1)

            def hidden_low(b, n):
                wait_for(dve, E["h_high"], FT, b, -1, n + 1)
                dve.tensor_tensor(h_lo[:, n, :], sil[:, n % 2, :], h_hi[:, n, :], ALU.subtract)\
                    .then_inc(E["h_low"], 1)

            def turn(b, prev, cur, nxt):
                for q in range(SLOTS):
                    if cur and q in (13, 23, 33, 43):
                        copy_max(b, q // 10 - 1)
                    if cur and q < NG * UNITS:
                        row_max(b, q // 10, q % 10)
                    if cur and q in (10, 20, 30, 40):
                        split_max(b, q // 10 - 1)
                    if prev and q == 3:
                        attn_norm(b, -1, NG - 1)
                    if prev and q in (6, 7):
                        low(b, -1, E["aT_high"], E["aT_low"], aT_lo, aT_hi, q - 6)
                    if prev and q in (9, 10):
                        i = q - 9
                        wait_for(dve, E["res_in"], 16, b, -1, 16)
                        wait_for(dve, E["wo_full"], 2, b, -1, i + 1)
                        dve.tensor_tensor(res[:, 2 * i:2 * i + 2, :],
                                          wk[:, i, :].rearrange("p (t d) -> p t d", t=2),
                                          res[:, 2 * i:2 * i + 2, :], ALU.add).then_inc(E["wo_out"], 1)
                    if prev and q == 10:
                        wait_for(dve, E["wo_out"], 2, b, -1, 2)
                        norm_stats(b, -1, res, st2, mv2, rs2, "2")
                    if prev and q == 12:
                        if cur:
                            wait_for(dve, E["x1T_full"], KT, b, 0, KT)
                        norm_apply(b, -1, xt, res, mv2, rs2, "2")
                    if prev and q in (15, 16):
                        low(b, -1, E["x2T_high"], E["x2T_low"], x2T_lo, x2T_hi, q - 15)
                    if prev and 16 <= q < 20:
                        for n in GATES[q - 16]:
                            hidden_full(b, n)
                            if n:
                                hidden_low(b, n - 1)
                    if prev and q == 20:
                        hidden_low(b, FT - 1)
                    if prev and q in (24, 25):
                        i = q - 24
                        wait_for(dve, E["y_full"], 2, b, -1, i + 1)
                        dve.scalar_tensor_tensor(out=res[:, 2 * i:2 * i + 2, :],
                                                 in0=wk[:, i, :].rearrange("p (t d) -> p t d", t=2), scalar=DEQ,
                                                 in1=res[:, 2 * i:2 * i + 2, :], op0=ALU.mult, op1=ALU.add)\
                            .then_inc(E["y_out"], 1)
                    if nxt and q == 25:
                        wait_for(dve, E["x_in"], 16, b, 1, 16)
                        norm_stats(b, 1, xt, st1, mv1, rs1, "1")
                    if nxt and q == 27:
                        norm_apply(b, 1, xt, xt, mv1, rs1, "1")
                    if cur and q in (35, 45, 55):
                        attn_norm(b, 0, q // 10 - 3)
                    if nxt and q in (38, 39):
                        low(b, 1, E["x1T_high"], E["x1T_low"], x1T_lo, x1T_hi, q - 38)
                    if nxt and q in (41, 44, 47, 50):
                        t = (q - 41) // 3
                        wait_for(dve, E["qk_full"], 4, b, 1, t + 1)
                        if t >= 2:
                            wait_for(dve, E["qk_low"], 4, b, 1, t - 1)
                        dve.tensor_tensor(rope[:, t % 2, 0, :], wk[:, t % 2, :], cos_sb[:, :], ALU.mult)\
                            .then_inc(E["qk_cos"], 1)
                        dve.stream_shuffle(rope[:, t % 2, 1, :], wk[:, t % 2, :], SWAP_PAIRS)\
                            .then_inc(E["qk_swap"], 2)
                    if nxt and q in (43, 46, 49, 52):
                        t = (q - 43) // 3
                        wait_for(dve, E["qk_hi"], 4, b, 1, t + 1)
                        dve.tensor_tensor(rope[:, t % 2, 0, :], rope[:, t % 2, 0, :], part[:, t % 2, 0, :],
                                          ALU.subtract).then_inc(E["qk_rest"], 1)
                    if nxt and q in (45, 48, 51, 54):
                        t = (q - 45) // 3
                        wait_for(dve, E["qk_mid"], 4, b, 1, t + 1)
                        dve.tensor_tensor(part[:, t % 2, 2, :], rope[:, t % 2, 0, :], part[:, t % 2, 1, :],
                                          ALU.subtract).then_inc(E["qk_low"], 1)

            dve.wait_ge(E["c_in"], 32)
            turns(dve, turn)

        @block.tensor
        def _(pe):
            def three(dst, k_tiles, w_hi, w_lo, m_hi, m_lo):
                for k in range(k_tiles):
                    pe.matmul(dst, w_hi(k), m_hi(k), start=k == 0, stop=False)
                    pe.matmul(dst, w_hi(k), m_lo(k), start=False, stop=False)
                    last = pe.matmul(dst, w_lo(k), m_hi(k), start=False, stop=k == k_tiles - 1)
                return last

            def project(n, w):
                return lambda k: w[:, k, P * n:P * (n + 1)]

            def tokens(i, a):
                return lambda k: a[:, k, P * i:P * (i + 1)]

            def turn_x(src, full, k):
                for i in range(TT):
                    last = pe.transpose(wk[:, k, P * i:P * (i + 1)], src[:, i, P * k:P * (k + 1)], ident[:, :])
                last.then_inc(full, 1)

            def turn_o(b, shift, g):
                wait_for(pe, E["o_copied"], NG, b, shift, g + 1)
                for i in range(TT):
                    last = pe.transpose(pvo[:, P * i:P * (i + 1)], oT[:, P * i:P * (i + 1)], ident[:, :])
                last.then_inc(E["o_turned"], 1)

            def scores_max(b, g, u):
                use, r, v = max_use(g, u), u // 5, u % 5
                bank = smax[:, use % 2, :]
                if u == 0 and g % 2 == 0:
                    wait_for(pe, E[f"stack_in{g // 2}"], 192, b, 1, 0)
                wait_for(pe, E["s_out"], S_USES, b, 0, use - 1)
                head = G * g + 2 * r + v // 2

                def score(h, i, at):
                    return pe.matmul(bank[:, at:at + P * (i + 1)], qs[0:STACK, h, P * i:P * (i + 1)],
                                     ks[0:STACK, h, 0:P * (i + 1)], start=False, stop=True,
                                     skip_group_check=True)

                if v == 4:
                    diag = bank.rearrange("p (k c) -> p k c", c=P)[:, 1:4:2, :]
                    pe.matmul(diag, identb[:, :], hide[:, :, :], start=True, stop=False, skip_group_check=True)
                    score(G * g + 2 * r, 1, 0)
                    last = score(G * g + 2 * r + 1, 1, 2 * P)
                elif v % 2 == 0:
                    pe.matmul(bank[:, 3 * P:S], identb[:, :], hide[:, 0, :], start=True, stop=False,
                              skip_group_check=True)
                    last = score(head, 3, 0)
                else:
                    pe.matmul(bank[:, 2 * P:S], identb[:, :], hide[:, :, :].rearrange("p k c -> p (k c)"),
                              start=True, stop=False, skip_group_check=True)
                    score(head, 2, 0)
                    last = score(head, 0, 3 * P)
                last.then_inc(E["s_full"], 1)

            def turn_max(b, g):
                use = turn_use(g)
                wait_for(pe, E["split"], NG, b, 0, g + 1)
                wait_for(pe, E["s_out"], S_USES, b, 0, use - 1)
                for i in range(TT):
                    last = pe.transpose(smax_b[0:G * MAXROWS, use % 2, P * i:P * (i + 1)],
                                        nmb[:, g, i, :, :].rearrange("p h n -> p (h n)"), identb[:, :])
                last.then_inc(E["s_full"], 1)

            def ring_free(b, shift, k):
                if k < 3:
                    wait_for(pe, E["t_out"], T_USES, b, shift - 1, T_LAST[k])
                else:
                    wait_for(pe, E["t_out"], T_USES, b, shift, k - 2)

            def scores_exp(b, g, u):
                k, r, v = UNITS * g + u, u // 5, u % 5
                bank = sexp[:, k % 3, :]
                if u == 0:
                    wait_for(pe, E[f"m_in{g}"], 64, b, 0, 64)
                ring_free(b, 0, k)
                rows = STACK + MAXROWS
                head = G * g + 2 * r + v // 2

                def score(h, j, at):
                    return pe.matmul(bank[:, at:at + S - P * j], ks[0:rows, h, P * j:P * (j + 1)],
                                     qs[0:rows, h, P * j:S], start=True, stop=True)

                if v == 4:
                    score(G * g + 2 * r, 2, 0)
                    last = score(G * g + 2 * r + 1, 2, 2 * P)
                elif v % 2 == 0:
                    last = score(head, 0, 0)
                else:
                    score(head, 1, 0)
                    last = score(head, 3, 3 * P)
                last.then_inc(E["t_full"], 1)

            def prob_values(b, shift, g):
                wait_for(pe, E["t_out"], T_USES, b, shift, UNITS * (g + 1))
                wait_for(pe, E["masked"], 16 * NG, b, shift, 16 * (g + 1))
                wait_for(pe, E["v_out"], 2, b, shift, 2)
                wait_for(pe, E["o_norm"], NG, b, shift, g)
                for j in range(TT):
                    for c in range(G):
                        u = 5 * (c // 2) + 2 * (c % 2)
                        p = (prob[:, u, :], prob[:, u + 1, 0:3 * P],
                             prob[:, 5 * (c // 2) + 4, 2 * P * (c % 2):2 * P * (c % 2 + 1)],
                             prob[:, u + 1, 3 * P:S])[j]
                        last = pe.matmul(pvo[32 * c:32 * (c + 1), P * j:S], vaug[:, j, G * g + c, :], p,
                                         start=j == 0, stop=j == TT - 1)
                last.then_inc(E["pv_full"], 1)

            def turn(b, prev, cur, nxt):
                for q in range(SLOTS):
                    if cur and q < NG * UNITS:
                        scores_max(b, q // 10, q % 10)
                    if cur and q in (12, 22, 32, 42):
                        turn_max(b, q // 10 - 1)
                    if cur and q >= 20:
                        scores_exp(b, (q - 20) // 10, q % 10)
                    if cur and q in (32, 42, 52):
                        prob_values(b, 0, q // 10 - 3)
                    if prev and q == 0:
                        prob_values(b, -1, NG - 1)
                    if prev and q == 2:
                        turn_o(b, -1, NG - 1)
                    if cur and q in (34, 44, 54):
                        turn_o(b, 0, q // 10 - 3)
                    if cur and q in (3, 4):
                        i = q - 3
                        wait_for(pe, E["qk_swap"], 8, b, 0, 2 * (i + 3))
                        for t in (2 * i, 2 * i + 1):
                            last = three(wk[:, i, D * (t % 2):D * (t % 2 + 1)], KT,
                                         tokens(t, x1T_hi), tokens(t, x1T_lo),
                                         lambda k: wqkv_hi[:, k, 2 * D:3 * D], lambda k: wqkv_lo[:, k, 2 * D:3 * D])
                        last.then_inc(E["v_full"], 1)
                    if prev and q in (5, 6):
                        wait_for(pe, E["o_norm"], NG, b, -1, NG)
                        if cur:
                            wait_for(pe, E["v_out"], 2, b, 0, q - 4)
                        else:
                            wait_for(pe, E["y_out"], 2, b, -2, q - 4)
                        k = q - 5
                        turn_x(attn[:, :, :, :].rearrange("p t h d -> p t (h d)"), E["aT_full"], k)
                    if prev and q in (8, 9):
                        i = q - 8
                        wait_for(pe, E["aT_low"], KT, b, -1, KT)
                        for t in (2 * i, 2 * i + 1):
                            last = three(wk[:, i, D * (t % 2):D * (t % 2 + 1)], KT,
                                         tokens(t, aT_hi), tokens(t, aT_lo),
                                         lambda k: wo_hi[:, k, :], lambda k: wo_lo[:, k, :])
                        last.then_inc(E["wo_full"], 1)
                    if prev and q in (14, 15):
                        wait_for(pe, E["norm2"], 1, b, -1, 1)
                        turn_x(xt, E["x2T_full"], q - 14)
                    if prev and 16 <= q < 20:
                        for n in GATES[q - 16]:
                            k = NG * UNITS + n
                            if n == 0:
                                wait_for(pe, E["x2T_low"], KT, b, -1, KT)
                            ring_free(b, -1, k)
                            three(sexp[:, k % 3, :], KT, project(n, wg_hi), project(n, wg_lo),
                                  lambda k: x2T_hi[:, k, :], lambda k: x2T_lo[:, k, :]).then_inc(E["t_full"], 1)
                            if n >= 2:
                                wait_for(pe, E["h_full"], FT, b, -1, n - 1)
                            three(wk[:, n % 2, :], KT, project(n, wu_hi), project(n, wu_lo),
                                  lambda k: x2T_hi[:, k, :], lambda k: x2T_lo[:, k, :]).then_inc(E["up_full"], 1)
                    if prev and q in (23, 24):
                        i = q - 23
                        wait_for(pe, E["h_low"], FT, b, -1, FT)
                        for t in (2 * i, 2 * i + 1):
                            last = three(wk[:, i, D * (t % 2):D * (t % 2 + 1)], FT,
                                         tokens(t, h_hi), tokens(t, h_lo),
                                         lambda k: wd_hi[:, k, :], lambda k: wd_lo[:, k, :])
                        last.then_inc(E["y_full"], 1)
                    if nxt and q in (36, 37):
                        i = q - 36
                        wait_for(pe, E["norm1"], 1, b, 1, 1)
                        if prev:
                            wait_for(pe, E["y_out"], 2, b, -1, i + 1)
                        elif cur:
                            wait_for(pe, E["v_out"], 2, b, 0, i + 1)
                        turn_x(xt, E["x1T_full"], i)
                    if nxt and q in (40, 43, 46, 49):
                        t = (q - 40) // 3
                        if t == 0:
                            wait_for(pe, E["x1T_low"], KT, b, 1, KT)
                        if t >= 2:
                            wait_for(pe, E["qk_swap"], 8, b, 1, 2 * (t - 1))
                        n = KT * (t % 2) + t // 2
                        three(wk[:, t % 2, :], KT, project(n, wqkv_hi), project(n, wqkv_lo),
                              lambda k: x1T_hi[:, k, :], lambda k: x1T_lo[:, k, :]).then_inc(E["qk_full"], 1)

            pe.wait_ge(E["iden"], 3)
            pe.wait_ge(E["w_lo"], 5)
            pe.wait_ge(E["hidden"], 2)
            pe.wait_ge(E["half_set"], 1)
            pe.wait_ge(E["ones_set"], 1)
            pe.wait_ge(E["vones"], 1)
            turns(pe, turn)


def kernel(L0_attn_x, L0_attn_Wq, L0_attn_Wk, L0_attn_Wv, L0_attn_Wo, L0_ffn_w_gate, L0_ffn_w_up, L0_ffn_w_down):
    import numpy as _np
    import concourse.bacc as _bacc
    from concourse import mybir as _mybir
    from concourse.bass_utils import run_bass_kernel_spmd as _run

    pos = _np.arange(S, dtype=_np.float32)
    inv_freq = (1.0 / _np.float32(10000.0) ** (_np.arange(0, DK, 2, dtype=_np.float32) / DK)).astype(_np.float32)
    angles = inv_freq[(_np.arange(P) % DK) // 2][:, None] * pos[None, :]
    sign = _np.where(_np.arange(P) % 2 == 0, -1.0, 1.0).astype(_np.float32)[:, None]
    arrays = {
        "x": _np.ascontiguousarray(L0_attn_x),
        "wqkv": _np.ascontiguousarray(_np.concatenate(
            [_np.transpose(_np.asarray(w)) for w in (L0_attn_Wq, L0_attn_Wk, L0_attn_Wv)], axis=1)),
        "wo": _np.ascontiguousarray(_np.transpose(_np.asarray(L0_attn_Wo))),
        "wg": _np.ascontiguousarray(_np.transpose(_np.asarray(L0_ffn_w_gate))),
        "wu": _np.ascontiguousarray(_np.transpose(_np.asarray(L0_ffn_w_up))),
        "wd": _np.ascontiguousarray(_np.transpose(_np.asarray(L0_ffn_w_down))),
        "cos_t": _np.cos(angles).astype(_np.float32),
        "sin_t": (sign * _np.sin(angles)).astype(_np.float32),
    }
    nc = _bacc.Bacc("TRN2", target_bir_lowering=False, num_devices=1)
    args = [nc.dram_tensor(n, a.shape, _mybir.dt.from_np(a.dtype), kind="ExternalInput").ap()
            for n, a in arrays.items()]
    args.append(nc.dram_tensor("out", (NB, S, D), _mybir.dt.float32, kind="ExternalOutput").ap())
    preln_block(nc, *args)
    r = _run(nc, [arrays], core_ids=[0])
    return r.results[0]["out"]
```

```python
from contextlib import ExitStack

import numpy as np

import concourse.bass as bass
from concourse import mybir

F32 = mybir.dt.float32
F32R = mybir.dt.float32r
BF16 = mybir.dt.bfloat16
I32 = mybir.dt.int32
ACT = mybir.ActivationFunctionType
ALU = mybir.AluOpType
AX = mybir.AxisListType

P = 128
NB = 8
S = 512
D = 256
H = 16
DK = D // H
HID = 768
TT = S // P
KT = D // P
FT = HID // P
G = 4
NG = H // G
UNITS = 10
TERMS_Q = (0, 0, 0, 1, 1, 2)
TERMS_K = (0, 1, 2, 0, 1, 0)
STACK = 16 * len(TERMS_Q)
MAXROWS = 2
EPS = 1e-5
DEQ = float(np.float32(1.0 / 127.0))
BELOW_ALL = -1e30
SLOTS = 6 * UNITS

PE_AT = dict(turn_max=(12, 22, 32, 42), pv=(31, 42, 51), pv_last=(4,), turn_o=(34, 44, 55), turn_o_last=(5,),
             v=(4, 6), aT=(6, 8), wo=(10, 11), x1T=(12, 13), qk=(15, 16, 20, 22), x2T=(27, 29),
             gate=(40, 41, 41, 41, 41, 41), down=(42, 50))
ACT_AT = dict(copy_o=(32, 43, 53), copy_o_last=(4,), v=(12, 14), aT=(12, 14), x1T=(14, 14),
              qk_hi=(17, 23, 25, 31), qk_mid=(17, 25, 27, 33), x2T=(30, 30), silu=(40, 40, 40, 40, 40, 40),
              h_high=(40, 40, 40, 40, 40, 40), weights=(19, 27, 35, 47))
DVE_AT = dict(stat1=(4,), apply1=(6,), norm_o=(41, 48, 54), norm_o_last=(5,), aT=(8, 8), wo=(10, 11),
              x1T=(13, 13), stat2=(14,), apply2=(17,), qk=(15, 18, 22, 27), qk_rest=(19, 23, 25, 33),
              x2T=(30, 30), h_full=(37, 40, 40, 40, 41, 42), h_low=(40, 40, 40, 41, 42, 44), y=(48, 53),
              weights=(23, 29, 42, 42))
POOL_AT = dict(root1=(14,), root2=(15,), rotate=(15, 16, 16, 29), qk_low=(15, 18, 23, 32))
SP_AT = dict(rows=(17, 18, 33, 41), store=(17, 20, 26, 35), load=(49,), out=(50,), res=(55,))

S_USES = NG * UNITS + NG
T_USES = NG * UNITS
T_LAST = {0: T_USES, 1: T_USES - 2, 2: T_USES - 1}
SWAP_PAIRS = [i ^ 1 for i in range(32)]


def wait_for(eng, sem, per, batch, shift, count):
    least = shift * per + count
    if isinstance(batch, int):
        if batch * per + least > 0:
            eng.wait_ge(sem, batch * per + least)
    else:
        assert per + least > 0
        eng.wait_ge(sem, batch * per + least)


def max_use(g, u):
    return UNITS * g + u + (g if u > 2 else max(g - 1, 0))


def turn_use(g):
    return UNITS * (g + 1) + 3 + g if g < NG - 1 else S_USES - 1


def preln_block(nc, x, wqkv, wo, wg, wu, wd, cos_t, sin_t, out):
    with ExitStack() as ctx:
        def sb(name, shape, dt):
            return ctx.enter_context(nc.sbuf_tensor(name, shape, dt))

        def pb(name, shape, dt):
            return ctx.enter_context(nc.psum_tensor(name, shape, dt))

        def sem(name):
            return ctx.enter_context(nc.semaphore(name))

        qs = sb("q_stack", [P, H, S], BF16)
        ks = sb("k_stack", [P, H, S], BF16)
        prob = sb("prob", [P, UNITS, S], F32)
        wqkv_hi, wqkv_lo = sb("wqkv_hi", [P, KT, 3 * D], F32R), sb("wqkv_lo", [P, KT, 3 * D], F32R)
        wo_hi, wo_lo = sb("wo_hi", [P, KT, D], F32R), sb("wo_lo", [P, KT, D], F32R)
        wg_hi, wg_lo = sb("wg_hi", [P, KT, HID], F32R), sb("wg_lo", [P, KT, HID], F32R)
        wu_hi, wu_lo = sb("wu_hi", [P, KT, HID], F32R), sb("wu_lo", [P, KT, HID], F32R)
        wd_hi, wd_lo = sb("wd_hi", [P, FT, D], F32R), sb("wd_lo", [P, FT, D], F32R)
        cos_sb, sin_sb = sb("cos_sb", [P, S], F32), sb("sin_sb", [P, S], F32)
        xt = sb("xt", [P, TT, D], F32)
        res = sb("res", [P, TT, D], F32)
        x1T_hi, x1T_lo = sb("x1T_hi", [P, KT, S], F32R), sb("x1T_lo", [P, KT, S], F32R)
        x2T_hi, x2T_lo = sb("x2T_hi", [P, KT, S], F32R), sb("x2T_lo", [P, KT, S], F32R)
        rope = sb("rope", [P, 2, 2, S], F32)
        part = sb("part", [P, 2, 3, S], BF16)
        vaug = sb("vaug", [P, TT, H, 32], F32)
        sil = sb("sil", [P, 2, S], F32)
        h_hi, h_lo = sb("h_hi", [P, FT, S], F32R), sb("h_lo", [P, FT, S], F32R)
        oT = sb("oT", [P, S], F32)
        rsum = sb("rsum", [P, TT, G, 1], F32)
        attn = sb("attn", [P, TT, H, DK], F32)
        aT_hi, aT_lo = sb("aT_hi", [P, KT, S], F32R), sb("aT_lo", [P, KT, S], F32R)
        nm = sb("neg_max", [P, NG, TT, G], F32)
        nmb = sb("neg_max_parts", [P, NG, TT, G, MAXROWS], BF16)
        mrow = sb("max_rows", [G * MAXROWS, 2, S], BF16)
        st1, mv1 = sb("st1", [P, TT, 6], F32), sb("mv1", [P, TT, 2], F32)
        st2, mv2 = sb("st2", [P, TT, 6], F32), sb("mv2", [P, TT, 2], F32)
        rs1, rs2 = sb("rs1", [P, 2, TT], F32), sb("rs2", [P, 2, TT], F32)
        minus_half = sb("minus_half", [P, TT], F32)
        ident, identb = sb("ident", [P, P], F32), sb("identb", [P, P], BF16)
        hide = sb("hide", [P, 2, P], BF16)

        smax = pb("smax", [P, 2, S], F32)
        sexp = pb("sexp", [P, 3, S], F32)
        pvo = pb("pvo", [P, S], F32)
        wk = pb("work", [P, 2, S], F32)
        smax_b = smax[:, :, :].bitcast(BF16)

        scr = nc.dram_tensor("parts", (4, 3, P, S), BF16, kind="Internal").ap()

        names = """wqkv_in wo_in wg_in wu_in wd_in c_in x_in res_in out_sent parts_sent0 parts_sent1 stack_in0 stack_in1
            m_in0 m_in1 m_in2 m_in3
            iden hidden ones_set half_set vones w_cast w_hi w_lo
            stat1 aggr1 var1 root1 norm1 stat2 aggr2 var2 root2 norm2
            x1T_full x1T_high x1T_low x2T_full x2T_high x2T_low
            qk_full qk_cos qk_swap qk_sin qk_rot qk_hi qk_rest qk_mid qk_low
            v_full v_out s_full s_out split_hi split t_full t_out masked
            pv_full o_copied o_turned o_inv o_norm aT_full aT_high aT_low wo_full wo_out
            gate_full sil_out up_full h_full h_high h_low y_full y_out""".split()
        E = {n: sem(n) for n in names}

        xv = x.rearrange("b (t p) d -> b p t d", p=P)
        ov = out.rearrange("b (t p) d -> b p t d", p=P)
        raw_f = rope[:, :, :, :].rearrange("p a b s -> p (a b s)")
        raw_i = prob[:, :, :].rearrange("p u s -> p (u s)")
        raw_qkv = raw_f[:, 0:KT * 3 * D].rearrange("p (k o) -> p k o", k=KT)
        raw_wo = attn[:, :, :, :].rearrange("p t h d -> p (t h d)")[:, 0:KT * D].rearrange("p (k o) -> p k o", k=KT)

        def raw_ffn(n, k):
            return raw_i[:, n * KT * HID:(n + 1) * KT * HID].rearrange("p (k o) -> p k o", k=k)

        block = ctx.enter_context(nc.Block())

        def at(steps, q):
            return [n for n, step in enumerate(steps) if step == q]

        def turns(eng, turn):
            turn(-1, False, False, True)
            turn(0, False, True, True)
            with eng.Fori(1, NB - 1) as b:
                turn(b, True, True, True)
            turn(NB - 1, True, True, False)
            turn(NB, True, False, False)

        @block.sync
        def _(sp):
            def max_rows(b, g):
                wait_for(sp, E["s_out"], S_USES, b, 0, turn_use(g) + 1)
                for j in range(G):
                    sp.dma_start(qs[STACK:STACK + MAXROWS, G * g + j, :],
                                 mrow[MAXROWS * j:MAXROWS * (j + 1), g % 2, :]).then_inc(E[f"m_in{g}"], 16)

            def store_parts(b, t):
                sp.dma_start(scr[t].rearrange("n r s -> r n s"), part[:, t % 2, :, :])\
                    .then_inc(E[f"parts_sent{t % 2}"], 16)

            def load_stack(b, t):
                dst, terms = ((qs, TERMS_Q), (ks, TERMS_K))[t % 2]
                for n, p in enumerate(terms):
                    sp.dma_start(dst[DK * n:DK * (n + 1), 8 * (t // 2):8 * (t // 2 + 1), :],
                                 scr[t, p].rearrange("(h d) s -> d h s", d=DK))\
                        .then_inc(E[f"stack_in{t // 2}"], 16)

            def turn(b, prev, cur, nxt):
                for q in range(SLOTS):
                    if q == 0:
                        wait_for(sp, E["t_full"], T_USES, b, 0, 0)
                        if nxt:
                            sp.dma_start(xt[:, :, :], xv[b + 1]).then_inc(E["x_in"], 16)
                        if cur:
                            load_stack(b, 2)
                            load_stack(b, 3)
                    for g in at(SP_AT["rows"], q):
                        if cur:
                            max_rows(b, g)
                    for t in at(SP_AT["store"], q):
                        if nxt:
                            wait_for(sp, E["qk_low"], 4, b, 1, t + 1)
                            store_parts(b, t)
                    for _ in at(SP_AT["load"], q):
                        if nxt:
                            for t in (0, 1):
                                wait_for(sp, E[f"parts_sent{t}"], 32, b, 1, 32)
                                load_stack(b, t)
                    for _ in at(SP_AT["out"], q):
                        if prev:
                            wait_for(sp, E["y_out"], KT, b, -1, 2)
                            sp.dma_start(ov[b - 1], res[:, :, :]).then_inc(E["out_sent"], 16)
                    for _ in at(SP_AT["res"], q):
                        if cur:
                            wait_for(sp, E["out_sent"], 16, b, -1, 16)
                            sp.dma_start(res[:, :, :], xv[b]).then_inc(E["res_in"], 16)

            sp.dma_start(raw_qkv, wqkv.rearrange("(k p) o -> p k o", p=P)).then_inc(E["wqkv_in"], 16)
            turns(sp, turn)
            wait_for(sp, E["out_sent"], 16, NB, 0, 0)

        @block.gpsimd
        def _(pool):
            pool.memset(ident[:, :], 0.0).then_inc(E["iden"], 1)
            pool.memset(hide[:, :, :], 0.0).then_inc(E["hidden"], 1)
            pool.memset(minus_half[:, :], -0.5).then_inc(E["half_set"], 1)
            pool.memset(vaug[:, :, :, DK:32], 1.0).then_inc(E["vones"], 1)
            pool.wait_ge(E["iden"], 1)
            pool.affine_select(out=ident[:, :], in_=ident[:, :], compare_op=ALU.not_equal, fill=1.0,
                               base=0, pattern=[[-1, P]], channel_multiplier=1).then_inc(E["iden"], 1)
            pool.wait_ge(E["hidden"], 1)
            pool.affine_select(out=hide[:, :, :], in_=hide[:, :, :], compare_op=ALU.is_ge,
                               fill=BELOW_ALL, base=0, pattern=[[0, 2], [-1, P]],
                               channel_multiplier=1).then_inc(E["hidden"], 1)

            def root(b, shift, rs, var, done):
                wait_for(pool, var, 1, b, shift, 1)
                pool.tensor_tensor(rs[:, 1, :], rs[:, 0, :], minus_half[:, :], ALU.pow).then_inc(done, 1)

            def keep(b, g, u):
                wait_for(pool, E["t_out"], T_USES, b, 0, UNITS * g + u + 1)
                if u % 5 == 2:
                    v = prob[:, u - 2:u + 1:2, 0:P]
                else:
                    v = prob[:, u, :].rearrange("p (k c) -> p k c", c=P)
                    v = v[:, 0:4:3, :] if u % 5 < 4 else v[:, 0:4:2, :]
                pool.affine_select(out=v, in_=v, compare_op=ALU.is_ge, fill=0.0, base=0,
                                   pattern=[[0, 2], [1, P]], channel_multiplier=-1).then_inc(E["masked"], 2)

            def rotate(b, t):
                wait_for(pool, E["qk_swap"], 8, b, 1, 2 * t + 2)
                pool.tensor_tensor(rope[:, t % 2, 1, :], rope[:, t % 2, 1, :], sin_sb[:, :], ALU.mult)\
                    .then_inc(E["qk_sin"], 1)
                wait_for(pool, E["qk_sin"], 4, b, 1, t + 1)
                pool.tensor_tensor(rope[:, t % 2, 0, :], rope[:, t % 2, 0, :], rope[:, t % 2, 1, :], ALU.add)\
                    .then_inc(E["qk_rot"], 1)

            def turn(b, prev, cur, nxt):
                for q in range(SLOTS):
                    if cur and q >= 20:
                        g, u = (q - 20) // 10, q % 10
                        if u % 5:
                            keep(b, g, u)
                    for _ in at(POOL_AT["root1"], q):
                        if nxt:
                            root(b, 1, rs1, E["var1"], E["root1"])
                    for _ in at(POOL_AT["root2"], q):
                        if prev:
                            root(b, -1, rs2, E["var2"], E["root2"])
                    for t in at(POOL_AT["rotate"], q):
                        if nxt:
                            rotate(b, t)
                    for t in at(POOL_AT["qk_low"], q):
                        if nxt:
                            wait_for(pool, E["qk_mid"], 4, b, 1, t + 1)
                            pool.tensor_tensor(part[:, t % 2, 2, :], rope[:, t % 2, 0, :], part[:, t % 2, 1, :],
                                               ALU.subtract).then_inc(E["qk_low"], 1)

            turns(pool, turn)

        @block.scalar
        def _(act):
            act.dma_start(cos_sb[:, :], cos_t).then_inc(E["c_in"], 16)
            act.dma_start(sin_sb[:, :], sin_t).then_inc(E["c_in"], 16)
            act.dma_start(raw_wo, wo.rearrange("(k p) o -> p k o", p=P)).then_inc(E["wo_in"], 16)
            act.dma_start(raw_ffn(0, KT).bitcast(I32), wg.rearrange("(k p) o -> p k o", p=P)).then_inc(E["wg_in"], 16)
            act.dma_start(raw_ffn(1, KT).bitcast(I32), wu.rearrange("(k p) o -> p k o", p=P)).then_inc(E["wu_in"], 16)
            act.dma_start(raw_ffn(2, FT).bitcast(I32), wd.rearrange("(k p) o -> p k o", p=P)).then_inc(E["wd_in"], 16)

            def weight_high(dst, src):
                act.activation(dst, src, ACT.Copy).then_inc(E["w_hi"], 1)

            act.wait_ge(E["wqkv_in"], 16)
            weight_high(wqkv_hi[:, :, :], raw_qkv)

            def other_weight_high(n):
                if n == 0:
                    act.wait_ge(E["wo_in"], 16)
                    weight_high(wo_hi[:, :, :], raw_wo)
                else:
                    act.wait_ge(E["w_cast"], n)
                    dst, k = ((wg_hi, KT), (wu_hi, KT), (wd_hi, FT))[n - 1]
                    weight_high(dst[:, :, :], raw_ffn(n - 1, k))

            def high(b, shift, full, done, dst, k):
                wait_for(act, full, KT, b, shift, k + 1)
                act.activation(dst[:, k, :], wk[:, k, :], ACT.Copy).then_inc(done, 1)

            def values(b, i):
                wait_for(act, E["v_full"], 2, b, 0, i + 1)
                wait_for(act, E["pv_full"], NG, b, -1, NG)
                act.activation(vaug[:, 2 * i:2 * i + 2, :, 0:DK],
                               wk[:, i, :].rearrange("p (t h d) -> p t h d", t=2, d=DK), ACT.Copy)\
                    .then_inc(E["v_out"], 1)

            def exps(b, g, u):
                k = UNITS * g + u
                wait_for(act, E["t_full"], T_USES, b, 0, k + 1)
                if u == 0:
                    wait_for(act, E["pv_full"], NG, b, 0, g)
                act.activation(prob[:, u, :], sexp[:, k % 3, :], ACT.Exp, scale=DK ** -0.5)\
                    .then_inc(E["t_out"], 1)

            def silu(b, n):
                wait_for(act, E["gate_full"], FT, b, -1, n + 1)
                if n >= 2:
                    wait_for(act, E["h_low"], FT, b, -1, n - 1)
                act.activation(sil[:, n % 2, :], wk[:, 0, :], ACT.Silu, scale=DEQ).then_inc(E["sil_out"], 1)

            def hidden_high(b, n):
                wait_for(act, E["h_full"], FT, b, -1, n + 1)
                act.activation(h_hi[:, n, :], sil[:, n % 2, :], ACT.Copy).then_inc(E["h_high"], 1)

            def copy_o(b, shift, g):
                wait_for(act, E["pv_full"], NG, b, shift, g + 1)
                wait_for(act, E["o_turned"], NG, b, shift, g)
                act.activation(oT[:, :], pvo[:, :], ACT.Copy).then_inc(E["o_copied"], 1)

            def turn(b, prev, cur, nxt):
                for q in range(SLOTS):
                    for _ in at(ACT_AT["copy_o_last"], q):
                        if prev:
                            copy_o(b, -1, NG - 1)
                    for g in at(ACT_AT["copy_o"], q):
                        if cur:
                            copy_o(b, 0, g)
                    for i in at(ACT_AT["v"], q):
                        if cur:
                            values(b, i)
                    for k in at(ACT_AT["aT"], q):
                        if prev:
                            high(b, -1, E["aT_full"], E["aT_high"], aT_hi, k)
                    for k in at(ACT_AT["x1T"], q):
                        if nxt:
                            high(b, 1, E["x1T_full"], E["x1T_high"], x1T_hi, k)
                    for k in at(ACT_AT["x2T"], q):
                        if prev:
                            high(b, -1, E["x2T_full"], E["x2T_high"], x2T_hi, k)
                    for n in range(FT):
                        if prev and ACT_AT["silu"][n] == q:
                            silu(b, n)
                        if prev and n and ACT_AT["h_high"][n - 1] == q:
                            hidden_high(b, n - 1)
                    if prev and ACT_AT["h_high"][FT - 1] == q:
                        hidden_high(b, FT - 1)
                    if cur and q >= 20:
                        exps(b, (q - 20) // 10, q % 10)
                    for t in at(ACT_AT["qk_hi"], q):
                        if nxt:
                            wait_for(act, E["qk_rot"], 4, b, 1, t + 1)
                            wait_for(act, E[f"parts_sent{t % 2}"], 32, b, 1, 16 * (t // 2))
                            act.activation(part[:, t % 2, 0, :], rope[:, t % 2, 0, :], ACT.Copy)\
                                .then_inc(E["qk_hi"], 1)
                    for t in at(ACT_AT["qk_mid"], q):
                        if nxt:
                            wait_for(act, E["qk_rest"], 4, b, 1, t + 1)
                            act.activation(part[:, t % 2, 1, :], rope[:, t % 2, 0, :], ACT.Copy)\
                                .then_inc(E["qk_mid"], 1)
                    for n in at(ACT_AT["weights"], q):
                        if not cur and not prev:
                            other_weight_high(n)

            turns(act, turn)

        @block.vector
        def _(dve):
            dve.memset(ks[STACK:STACK + MAXROWS, :, :], 1.0).then_inc(E["ones_set"], 1)
            def weight_low(dst, src, hi, n):
                dve.wait_ge(E["w_hi"], n + 1)
                dve.tensor_tensor(dst, src, hi, ALU.subtract).then_inc(E["w_lo"], 1)

            dve.wait_ge(E["iden"], 2)
            dve.tensor_copy(identb[:, :], ident[:, :]).then_inc(E["iden"], 1)
            weight_low(wqkv_lo[:, :, :], raw_qkv, wqkv_hi[:, :, :], 0)

            def weight_cast(n):
                dve.wait_ge(E[("wg_in", "wu_in", "wd_in")[n]], 16)
                raw = raw_ffn(n, FT if n == 2 else KT)
                dve.tensor_copy(raw, raw.bitcast(I32)).then_inc(E["w_cast"], 1)

            def other_weight_low(n):
                if n == 0:
                    weight_low(wo_lo[:, :, :], raw_wo, wo_hi[:, :, :], 1)
                    for k in range(3):
                        weight_cast(k)
                else:
                    dst, hi, k = ((wg_lo, wg_hi, KT), (wu_lo, wu_hi, KT), (wd_lo, wd_hi, FT))[n - 1]
                    dve.wait_ge(E["w_cast"], n)
                    weight_low(dst[:, :, :], raw_ffn(n - 1, k), hi[:, :, :], n + 1)

            def norm_stats(b, shift, src, st, mv, rs, which):
                for i in range(TT):
                    last = dve.bn_stats(st[:, i, :], src[:, i, :])
                last.then_inc(E["stat" + which], 1)
                wait_for(dve, E["stat" + which], 1, b, shift, 1)
                for i in range(TT):
                    dve.bn_aggr(mv[:, i, :], st[:, i, :]).then_inc(E["aggr" + which], 2)
                wait_for(dve, E["aggr" + which], 2 * TT, b, shift, 2 * TT)
                dve.tensor_scalar(rs[:, 0, :], mv[:, :, 1], EPS, None, ALU.add).then_inc(E["var" + which], 1)

            def norm_apply(b, shift, dst, src, mv, rs, which):
                wait_for(dve, E["root" + which], 1, b, shift, 1)
                for i in range(TT):
                    last = dve.tensor_scalar(dst[:, i, :], src[:, i, :], mv[:, i, 0:1], rs[:, 1, i:i + 1],
                                             ALU.subtract, ALU.mult)
                last.then_inc(E["norm" + which], 1)

            def low(b, shift, high, done, dst, hi, k):
                wait_for(dve, high, KT, b, shift, k + 1)
                dve.tensor_tensor(dst[:, k, :], wk[:, k, :], hi[:, k, :], ALU.subtract).then_inc(done, 1)

            def row_max(b, g, u):
                use, r, v = max_use(g, u), u // 5, u % 5
                bank = smax[:, use % 2, :]
                wait_for(dve, E["s_full"], S_USES, b, 0, use + 1)
                if v == 4:
                    last = dve.tensor_reduce(nm[:, g, 1, 2 * r:2 * r + 2],
                                             bank.rearrange("p (h c) -> p h c", h=2), AX.X, ALU.max, negate=True)
                else:
                    h = 2 * r + v // 2
                    if v % 2 == 0:
                        last = dve.tensor_reduce(nm[:, g, 3, h:h + 1], bank, AX.X, ALU.max, negate=True)
                    else:
                        dve.tensor_reduce(nm[:, g, 2, h:h + 1], bank[:, 0:3 * P], AX.X, ALU.max, negate=True)
                        last = dve.tensor_reduce(nm[:, g, 0, h:h + 1], bank[:, 3 * P:S], AX.X, ALU.max, negate=True)
                last.then_inc(E["s_out"], 1)

            def split_max(b, g):
                wait_for(dve, E["s_out"], S_USES, b, 0, max_use(g, UNITS - 1) + 1)
                dve.tensor_copy(nmb[:, g, :, :, 0], nm[:, g, :, :]).then_inc(E["split_hi"], 1)
                wait_for(dve, E["split_hi"], NG, b, 0, g + 1)
                dve.tensor_tensor(nmb[:, g, :, :, 1], nm[:, g, :, :], nmb[:, g, :, :, 0], ALU.subtract)\
                    .then_inc(E["split"], 1)

            def copy_max(b, g):
                use = turn_use(g)
                wait_for(dve, E["s_full"], S_USES, b, 0, use + 1)
                if g < 2:
                    wait_for(dve, E[f"m_in{g + 2}"], 64, b, -1, 64)
                else:
                    wait_for(dve, E[f"m_in{g - 2}"], 64, b, 0, 64)
                dve.tensor_copy(mrow[:, g % 2, :], smax_b[0:G * MAXROWS, use % 2, 0:S])\
                    .then_inc(E["s_out"], 1)

            def attn_norm(b, shift, g):
                o = pvo[:, :].rearrange("p (t h c) -> p t h c", t=TT, h=G)
                wait_for(dve, E["o_turned"], NG, b, shift, g + 1)
                dve.reciprocal(rsum[:, :, :, :], o[:, :, :, DK:DK + 1]).then_inc(E["o_inv"], 1)
                wait_for(dve, E["o_inv"], NG, b, shift, g + 1)
                if g == 0:
                    wait_for(dve, E["aT_full"], KT, b, shift - 1, KT)
                dve.tensor_tensor(attn[:, :, G * g:G * (g + 1), :], o[:, :, :, 0:DK],
                                  rsum[:, :, :, :].broadcast_to([P, TT, G, DK]), ALU.mult)\
                    .then_inc(E["o_norm"], 1)

            def hidden_full(b, n):
                wait_for(dve, E["up_full"], FT, b, -1, n + 1)
                wait_for(dve, E["sil_out"], FT, b, -1, n + 1)
                dve.scalar_tensor_tensor(out=sil[:, n % 2, :], in0=wk[:, 1, :], scalar=DEQ,
                                         in1=sil[:, n % 2, :], op0=ALU.mult, op1=ALU.mult)\
                    .then_inc(E["h_full"], 1)

            def hidden_low(b, n):
                wait_for(dve, E["h_high"], FT, b, -1, n + 1)
                dve.tensor_tensor(h_lo[:, n, :], sil[:, n % 2, :], h_hi[:, n, :], ALU.subtract)\
                    .then_inc(E["h_low"], 1)

            def turn(b, prev, cur, nxt):
                for q in range(SLOTS):
                    for g in at(PE_AT["turn_max"], q - 1):
                        if cur:
                            copy_max(b, g)
                    if cur and q < NG * UNITS:
                        row_max(b, q // 10, q % 10)
                    if cur and q in (10, 20, 30, 40):
                        split_max(b, q // 10 - 1)
                    for _ in at(DVE_AT["norm_o_last"], q):
                        if prev:
                            attn_norm(b, -1, NG - 1)
                    for g in at(DVE_AT["norm_o"], q):
                        if cur:
                            attn_norm(b, 0, g)
                    for _ in at(DVE_AT["stat1"], q):
                        if nxt:
                            wait_for(dve, E["x_in"], 16, b, 1, 16)
                            norm_stats(b, 1, xt, st1, mv1, rs1, "1")
                    for _ in at(DVE_AT["apply1"], q):
                        if nxt:
                            norm_apply(b, 1, xt, xt, mv1, rs1, "1")
                    for k in at(DVE_AT["aT"], q):
                        if prev:
                            low(b, -1, E["aT_high"], E["aT_low"], aT_lo, aT_hi, k)
                    for i in at(DVE_AT["wo"], q):
                        if prev:
                            wait_for(dve, E["res_in"], 16, b, -1, 16)
                            wait_for(dve, E["wo_full"], 2, b, -1, i + 1)
                            dve.tensor_tensor(res[:, 2 * i:2 * i + 2, :],
                                              wk[:, i, :].rearrange("p (t d) -> p t d", t=2),
                                              res[:, 2 * i:2 * i + 2, :], ALU.add).then_inc(E["wo_out"], 1)
                    for k in at(DVE_AT["x1T"], q):
                        if nxt:
                            low(b, 1, E["x1T_high"], E["x1T_low"], x1T_lo, x1T_hi, k)
                    for _ in at(DVE_AT["stat2"], q):
                        if prev:
                            wait_for(dve, E["wo_out"], 2, b, -1, 2)
                            norm_stats(b, -1, res, st2, mv2, rs2, "2")
                    for _ in at(DVE_AT["apply2"], q):
                        if prev:
                            norm_apply(b, -1, xt, res, mv2, rs2, "2")
                    for t in at(DVE_AT["qk"], q):
                        if nxt:
                            wait_for(dve, E["qk_full"], 4, b, 1, t + 1)
                            if t % 2 == 0:
                                wait_for(dve, E[f"stack_in{t // 2}"], 192, b, 1, 0)
                            if t >= 2:
                                wait_for(dve, E["qk_low"], 4, b, 1, t - 1)
                            dve.tensor_tensor(rope[:, t % 2, 0, :], wk[:, t % 2, :], cos_sb[:, :], ALU.mult)\
                                .then_inc(E["qk_cos"], 1)
                            dve.stream_shuffle(rope[:, t % 2, 1, :], wk[:, t % 2, :], SWAP_PAIRS)\
                                .then_inc(E["qk_swap"], 2)
                    for t in at(DVE_AT["qk_rest"], q):
                        if nxt:
                            wait_for(dve, E["qk_hi"], 4, b, 1, t + 1)
                            dve.tensor_tensor(rope[:, t % 2, 0, :], rope[:, t % 2, 0, :], part[:, t % 2, 0, :],
                                              ALU.subtract).then_inc(E["qk_rest"], 1)
                    for k in at(DVE_AT["x2T"], q):
                        if prev:
                            low(b, -1, E["x2T_high"], E["x2T_low"], x2T_lo, x2T_hi, k)
                    for n in range(FT):
                        if prev and DVE_AT["h_full"][n] == q:
                            hidden_full(b, n)
                        if prev and n and DVE_AT["h_low"][n - 1] == q:
                            hidden_low(b, n - 1)
                    if prev and DVE_AT["h_low"][FT - 1] == q:
                        hidden_low(b, FT - 1)
                    for i in at(DVE_AT["y"], q):
                        if prev:
                            wait_for(dve, E["y_full"], 2, b, -1, i + 1)
                            dve.scalar_tensor_tensor(out=res[:, 2 * i:2 * i + 2, :],
                                                     in0=wk[:, i, :].rearrange("p (t d) -> p t d", t=2), scalar=DEQ,
                                                     in1=res[:, 2 * i:2 * i + 2, :], op0=ALU.mult, op1=ALU.add)\
                                .then_inc(E["y_out"], 1)
                    for n in at(DVE_AT["weights"], q):
                        if not cur and not prev:
                            other_weight_low(n)

            dve.wait_ge(E["c_in"], 32)
            turns(dve, turn)

        @block.tensor
        def _(pe):
            def three(dst, k_tiles, w_hi, w_lo, m_hi, m_lo):
                for k in range(k_tiles):
                    pe.matmul(dst, w_hi(k), m_hi(k), start=k == 0, stop=False)
                    pe.matmul(dst, w_hi(k), m_lo(k), start=False, stop=False)
                    last = pe.matmul(dst, w_lo(k), m_hi(k), start=False, stop=k == k_tiles - 1)
                return last

            def project(n, w):
                return lambda k: w[:, k, P * n:P * (n + 1)]

            def tokens(i, a):
                return lambda k: a[:, k, P * i:P * (i + 1)]

            def turn_x(src, full, k):
                for i in range(TT):
                    last = pe.transpose(wk[:, k, P * i:P * (i + 1)], src[:, i, P * k:P * (k + 1)], ident[:, :])
                last.then_inc(full, 1)

            def turn_o(b, shift, g):
                wait_for(pe, E["o_copied"], NG, b, shift, g + 1)
                for i in range(TT):
                    last = pe.transpose(pvo[:, P * i:P * (i + 1)], oT[:, P * i:P * (i + 1)], ident[:, :])
                last.then_inc(E["o_turned"], 1)

            def scores_max(b, g, u):
                use, r, v = max_use(g, u), u // 5, u % 5
                bank = smax[:, use % 2, :]
                if u == 0 and g % 2 == 0:
                    wait_for(pe, E[f"stack_in{g // 2}"], 192, b, 1, 0)
                wait_for(pe, E["s_out"], S_USES, b, 0, use - 1)
                head = G * g + 2 * r + v // 2

                def score(h, i, at):
                    return pe.matmul(bank[:, at:at + P * (i + 1)], qs[0:STACK, h, P * i:P * (i + 1)],
                                     ks[0:STACK, h, 0:P * (i + 1)], start=False, stop=True,
                                     skip_group_check=True)

                if v == 4:
                    diag = bank.rearrange("p (k c) -> p k c", c=P)[:, 1:4:2, :]
                    pe.matmul(diag, identb[:, :], hide[:, :, :], start=True, stop=False, skip_group_check=True)
                    score(G * g + 2 * r, 1, 0)
                    last = score(G * g + 2 * r + 1, 1, 2 * P)
                elif v % 2 == 0:
                    pe.matmul(bank[:, 3 * P:S], identb[:, :], hide[:, 0, :], start=True, stop=False,
                              skip_group_check=True)
                    last = score(head, 3, 0)
                else:
                    pe.matmul(bank[:, 2 * P:S], identb[:, :], hide[:, :, :].rearrange("p k c -> p (k c)"),
                              start=True, stop=False, skip_group_check=True)
                    score(head, 2, 0)
                    last = score(head, 0, 3 * P)
                last.then_inc(E["s_full"], 1)

            def turn_max(b, g):
                use = turn_use(g)
                wait_for(pe, E["split"], NG, b, 0, g + 1)
                wait_for(pe, E["s_out"], S_USES, b, 0, use - 1)
                for i in range(TT):
                    last = pe.transpose(smax_b[0:G * MAXROWS, use % 2, P * i:P * (i + 1)],
                                        nmb[:, g, i, :, :].rearrange("p h n -> p (h n)"), identb[:, :])
                last.then_inc(E["s_full"], 1)

            def ring_free(b, shift, k):
                if k < 3:
                    wait_for(pe, E["t_out"], T_USES, b, shift - 1, T_LAST[k])
                else:
                    wait_for(pe, E["t_out"], T_USES, b, shift, k - 2)

            def scores_exp(b, g, u):
                k, r, v = UNITS * g + u, u // 5, u % 5
                bank = sexp[:, k % 3, :]
                if u == 0:
                    wait_for(pe, E[f"m_in{g}"], 64, b, 0, 64)
                ring_free(b, 0, k)
                rows = STACK + MAXROWS
                head = G * g + 2 * r + v // 2

                def score(h, j, at):
                    return pe.matmul(bank[:, at:at + S - P * j], ks[0:rows, h, P * j:P * (j + 1)],
                                     qs[0:rows, h, P * j:S], start=True, stop=True)

                if v == 4:
                    score(G * g + 2 * r, 2, 0)
                    last = score(G * g + 2 * r + 1, 2, 2 * P)
                elif v % 2 == 0:
                    last = score(head, 0, 0)
                else:
                    score(head, 1, 0)
                    last = score(head, 3, 3 * P)
                last.then_inc(E["t_full"], 1)

            def prob_values(b, shift, g):
                wait_for(pe, E["t_out"], T_USES, b, shift, UNITS * (g + 1))
                wait_for(pe, E["masked"], 16 * NG, b, shift, 16 * (g + 1))
                wait_for(pe, E["v_out"], 2, b, shift, 2)
                wait_for(pe, E["o_norm"], NG, b, shift, g)
                for j in range(TT):
                    for c in range(G):
                        u = 5 * (c // 2) + 2 * (c % 2)
                        p = (prob[:, u, :], prob[:, u + 1, 0:3 * P],
                             prob[:, 5 * (c // 2) + 4, 2 * P * (c % 2):2 * P * (c % 2 + 1)],
                             prob[:, u + 1, 3 * P:S])[j]
                        last = pe.matmul(pvo[32 * c:32 * (c + 1), P * j:S], vaug[:, j, G * g + c, :], p,
                                         start=j == 0, stop=j == TT - 1)
                last.then_inc(E["pv_full"], 1)

            def gate_up(b, n):
                if n == 0:
                    wait_for(pe, E["x2T_low"], KT, b, -1, KT)
                else:
                    wait_for(pe, E["sil_out"], FT, b, -1, n)
                three(wk[:, 0, :], KT, project(n, wg_hi), project(n, wg_lo),
                      lambda k: x2T_hi[:, k, :], lambda k: x2T_lo[:, k, :]).then_inc(E["gate_full"], 1)
                if n:
                    wait_for(pe, E["h_full"], FT, b, -1, n)
                three(wk[:, 1, :], KT, project(n, wu_hi), project(n, wu_lo),
                      lambda k: x2T_hi[:, k, :], lambda k: x2T_lo[:, k, :]).then_inc(E["up_full"], 1)

            def turn(b, prev, cur, nxt):
                for q in range(SLOTS):
                    if cur and q < NG * UNITS:
                        scores_max(b, q // 10, q % 10)
                    for g in at(PE_AT["turn_max"], q):
                        if cur:
                            turn_max(b, g)
                    if cur and q >= 20:
                        scores_exp(b, (q - 20) // 10, q % 10)
                    for g in at(PE_AT["pv"], q):
                        if cur:
                            prob_values(b, 0, g)
                    for _ in at(PE_AT["pv_last"], q):
                        if prev:
                            prob_values(b, -1, NG - 1)
                    for _ in at(PE_AT["turn_o_last"], q):
                        if prev:
                            turn_o(b, -1, NG - 1)
                    for g in at(PE_AT["turn_o"], q):
                        if cur:
                            turn_o(b, 0, g)
                    for i in at(PE_AT["v"], q):
                        if cur:
                            if prev:
                                wait_for(pe, E["o_norm"], NG, b, -1, NG - 1)
                            else:
                                wait_for(pe, E["qk_swap"], 8, b, 0, 2 * (i + 3))
                            for t in (2 * i, 2 * i + 1):
                                last = three(wk[:, i, D * (t % 2):D * (t % 2 + 1)], KT,
                                             tokens(t, x1T_hi), tokens(t, x1T_lo),
                                             lambda k: wqkv_hi[:, k, 2 * D:3 * D], lambda k: wqkv_lo[:, k, 2 * D:3 * D])
                            last.then_inc(E["v_full"], 1)
                    for k in at(PE_AT["aT"], q):
                        if prev:
                            wait_for(pe, E["o_norm"], NG, b, -1, NG)
                            if cur:
                                wait_for(pe, E["v_out"], 2, b, 0, k + 1)
                            turn_x(attn[:, :, :, :].rearrange("p t h d -> p t (h d)"), E["aT_full"], k)
                    for i in at(PE_AT["wo"], q):
                        if prev:
                            wait_for(pe, E["aT_low"], KT, b, -1, KT)
                            for t in (2 * i, 2 * i + 1):
                                last = three(wk[:, i, D * (t % 2):D * (t % 2 + 1)], KT,
                                             tokens(t, aT_hi), tokens(t, aT_lo),
                                             lambda k: wo_hi[:, k, :], lambda k: wo_lo[:, k, :])
                            last.then_inc(E["wo_full"], 1)
                    for k in at(PE_AT["x1T"], q):
                        if nxt:
                            wait_for(pe, E["norm1"], 1, b, 1, 1)
                            if prev:
                                wait_for(pe, E["wo_out"], 2, b, -1, k + 1)
                            elif cur:
                                wait_for(pe, E["v_out"], 2, b, 0, k + 1)
                            turn_x(xt, E["x1T_full"], k)
                    for t in at(PE_AT["qk"], q):
                        if nxt:
                            if t == 0:
                                wait_for(pe, E["x1T_low"], KT, b, 1, KT)
                            if t >= 2:
                                wait_for(pe, E["qk_swap"], 8, b, 1, 2 * (t - 1))
                            n = KT * (t % 2) + t // 2
                            three(wk[:, t % 2, :], KT, project(n, wqkv_hi), project(n, wqkv_lo),
                                  lambda k: x1T_hi[:, k, :], lambda k: x1T_lo[:, k, :]).then_inc(E["qk_full"], 1)
                    for k in at(PE_AT["x2T"], q):
                        if prev:
                            wait_for(pe, E["norm2"], 1, b, -1, 1)
                            if nxt:
                                wait_for(pe, E["qk_swap"], 8, b, 1, 2 * (k + 3))
                            turn_x(xt, E["x2T_full"], k)
                    for n in at(PE_AT["gate"], q):
                        if prev:
                            gate_up(b, n)
                    for i in at(PE_AT["down"], q):
                        if prev:
                            wait_for(pe, E["h_low"], FT, b, -1, FT)
                            for t in (2 * i, 2 * i + 1):
                                last = three(wk[:, i, D * (t % 2):D * (t % 2 + 1)], FT,
                                             tokens(t, h_hi), tokens(t, h_lo),
                                             lambda k: wd_hi[:, k, :], lambda k: wd_lo[:, k, :])
                            last.then_inc(E["y_full"], 1)
                    if not prev and not cur and q == SLOTS - 1:
                        pe.wait_ge(E["w_lo"], 5)
                        pe.wait_ge(E["hidden"], 2)
                        pe.wait_ge(E["ones_set"], 1)
                        pe.wait_ge(E["vones"], 1)

            pe.wait_ge(E["iden"], 3)
            pe.wait_ge(E["w_lo"], 1)
            turns(pe, turn)


def kernel(L0_attn_x, L0_attn_Wq, L0_attn_Wk, L0_attn_Wv, L0_attn_Wo, L0_ffn_w_gate, L0_ffn_w_up, L0_ffn_w_down):
    import numpy as _np
    import concourse.bacc as _bacc
    from concourse import mybir as _mybir
    from concourse.bass_utils import run_bass_kernel_spmd as _run

    pos = _np.arange(S, dtype=_np.float32)
    inv_freq = (1.0 / _np.float32(10000.0) ** (_np.arange(0, DK, 2, dtype=_np.float32) / DK)).astype(_np.float32)
    angles = inv_freq[(_np.arange(P) % DK) // 2][:, None] * pos[None, :]
    sign = _np.where(_np.arange(P) % 2 == 0, -1.0, 1.0).astype(_np.float32)[:, None]
    arrays = {
        "x": _np.ascontiguousarray(L0_attn_x),
        "wqkv": _np.ascontiguousarray(_np.concatenate(
            [_np.transpose(_np.asarray(w)) for w in (L0_attn_Wq, L0_attn_Wk, L0_attn_Wv)], axis=1)),
        "wo": _np.ascontiguousarray(_np.transpose(_np.asarray(L0_attn_Wo))),
        "wg": _np.ascontiguousarray(_np.transpose(_np.asarray(L0_ffn_w_gate))),
        "wu": _np.ascontiguousarray(_np.transpose(_np.asarray(L0_ffn_w_up))),
        "wd": _np.ascontiguousarray(_np.transpose(_np.asarray(L0_ffn_w_down))),
        "cos_t": _np.cos(angles).astype(_np.float32),
        "sin_t": (sign * _np.sin(angles)).astype(_np.float32),
    }
    nc = _bacc.Bacc("TRN2", target_bir_lowering=False, num_devices=1)
    args = [nc.dram_tensor(n, a.shape, _mybir.dt.from_np(a.dtype), kind="ExternalInput").ap()
            for n, a in arrays.items()]
    args.append(nc.dram_tensor("out", (NB, S, D), _mybir.dt.float32, kind="ExternalOutput").ap())
    preln_block(nc, *args)
    r = _run(nc, [arrays], core_ids=[0])
    return r.results[0]["out"]
```

```python
from contextlib import ExitStack

import numpy as np

import concourse.bass as bass
from concourse import mybir

F32 = mybir.dt.float32
F32R = mybir.dt.float32r
BF16 = mybir.dt.bfloat16
I32 = mybir.dt.int32
ACT = mybir.ActivationFunctionType
ALU = mybir.AluOpType
AX = mybir.AxisListType

P = 128
NB = 8
S = 512
D = 256
H = 16
DK = D // H
HID = 768
TT = S // P
KT = D // P
FT = HID // P
G = 4
NG = H // G
UNITS = 10
SINGLE_Q = (0, 0, 1)
SINGLE_K = (0, 1, 0)
STACK = DK * (3 + len(SINGLE_Q))
MAXROWS = 2
EPS = 1e-5
DEQ = float(np.float32(1.0 / 127.0))
BELOW_ALL = -1e30
MAX_BANKS = 3
EXP_BANKS = 2
SIL_SLOTS = 3
SLOTS = 72
MAX_STEPS = 61
EXP_STEP = 35
GAP_FROM = 10
EXP_GAP = 8
TURN_AFTER = 5

PE_AT = dict(turn_max=(63,), pv=(52, 64, 73, 86), turn_o=(60, 66, 83, 90), v=(14, 18), aT=(19, 19),
             wo=(23, 24), x1T=(26, 26), qk=(30, 30, 34, 34), x2T=(40, 40), gate=(44, 49, 50, 50, 50, 51),
             down=(54, 64))
ACT_AT = dict(copy_o=(53, 65, 79, 84), v=(19, 19), aT=(19, 25), x1T=(29, 31), qk_hi=(32, 32, 42, 45),
              qk_mid=(33, 35, 47, 48), x2T=(41, 41), silu=(45, 46, 48, 50, 51, 51),
              h_high=(48, 50, 51, 51, 51, 51))
DVE_AT = dict(split=(13, 31, 52, 62), copy_max=(64,), stat1=(3,), apply1=(13,), norm_o=(63, 72, 81, 88),
              aT=(19, 19), wo=(24, 24), x1T=(25, 25), stat2=(25,), apply2=(37,), qk=(26, 29, 37, 37),
              x2T=(40, 40), h_full=(45, 46, 49, 50, 50, 50), y=(71, 71))
POOL_AT = dict(root1=(4,), root2=(12,), rotate=(12, 16, 36, 36), qk_rest=(17, 27, 37, 45),
               qk_low=(28, 33, 46, 50), h_low=(45, 46, 47, 52, 52, 53))
SP_AT = dict(rows=(11, 21, 39, 52), store=(12, 13, 22, 38), load_first=(46,), load_last=(10,), out=(58,),
             res=(67,))

PE_START = dict(x1T=(16, 16), qk=(18, 18, 56, 65))
ACT_START = dict(x1T=(12, 12), qk_hi=(22, 25, 34, 36), qk_mid=(33, 33, 36, 44), weights=(3, 17, 35, 47, 50))
DVE_START = dict(stat1=(0,), apply1=(10,), x1T=(13, 13), qk=(30, 35, 44, 56), cast=(29, 58, 74),
                 weights=(9, 34, 66, 98, 105))
POOL_START = dict(root1=(6,), rotate=(8, 16, 26, 31), qk_rest=(18, 20, 33, 35), qk_low=(22, 23, 43, 51))
SP_START = dict(store=(8, 9, 27, 63), load_first=(18,))

S_USES = NG * UNITS + NG
T_USES = NG * UNITS
SWAP_PAIRS = [i ^ 1 for i in range(32)]


def wait_for(eng, sem, per, batch, shift, count):
    least = shift * per + count
    if isinstance(batch, int):
        if batch * per + least > 0:
            eng.wait_ge(sem, batch * per + least)
    else:
        assert per + least > 0
        eng.wait_ge(sem, batch * per + least)


def ring_free(eng, sem, uses, banks, batch, shift, k):
    if k < banks:
        wait_for(eng, sem, uses, batch, shift - 1, uses - (uses - 1 - k) % banks)
    else:
        wait_for(eng, sem, uses, batch, shift, k - banks + 1)


def max_step(g, u):
    return (UNITS * g + u) * MAX_STEPS // (NG * UNITS)


def max_use(g, u):
    return UNITS * g + u + (g if u > TURN_AFTER else max(g - 1, 0))


def turn_use(g):
    return UNITS * (g + 1) + TURN_AFTER + 1 + g if g < NG - 1 else S_USES - 1


def preln_block(nc, x, wqkv, wo, wg, wu, wd, cos_t, sin_t, out):
    with ExitStack() as ctx:
        def sb(name, shape, dt):
            return ctx.enter_context(nc.sbuf_tensor(name, shape, dt))

        def pb(name, shape, dt):
            return ctx.enter_context(nc.psum_tensor(name, shape, dt))

        def sem(name):
            return ctx.enter_context(nc.semaphore(name))

        qs = sb("q_stack", [P, H, S], BF16)
        ks = sb("k_stack", [P, H, S], BF16)
        prob = sb("prob", [P, UNITS, S], F32)
        wqkv_hi, wqkv_lo = sb("wqkv_hi", [P, KT, 3 * D], F32R), sb("wqkv_lo", [P, KT, 3 * D], F32R)
        wo_hi, wo_lo = sb("wo_hi", [P, KT, D], F32R), sb("wo_lo", [P, KT, D], F32R)
        wg_hi, wg_lo = sb("wg_hi", [P, KT, HID], F32R), sb("wg_lo", [P, KT, HID], F32R)
        wu_hi, wu_lo = sb("wu_hi", [P, KT, HID], F32R), sb("wu_lo", [P, KT, HID], F32R)
        wd_hi, wd_lo = sb("wd_hi", [P, FT, D], F32R), sb("wd_lo", [P, FT, D], F32R)
        cos_sb, sin_sb = sb("cos_sb", [P, S], F32), sb("sin_sb", [P, S], F32)
        xt = sb("xt", [P, TT, D], F32)
        res = sb("res", [P, TT, D], F32)
        x1T_hi, x1T_lo = sb("x1T_hi", [P, KT, S], F32R), sb("x1T_lo", [P, KT, S], F32R)
        x2T_hi, x2T_lo = sb("x2T_hi", [P, KT, S], F32R), sb("x2T_lo", [P, KT, S], F32R)
        rope = sb("rope", [P, 2, 2, S], F32)
        part = sb("part", [P, 2, 3, S], BF16)
        vaug = sb("vaug", [P, TT, H, 32], F32)
        sil = sb("sil", [P, SIL_SLOTS, S], F32)
        h_hi, h_lo = sb("h_hi", [P, FT, S], F32R), sb("h_lo", [P, FT, S], F32R)
        oT = sb("oT", [P, S], F32)
        rsum = sb("rsum", [P, TT, G, 1], F32)
        attn = sb("attn", [P, TT, H, DK], F32)
        aT_hi, aT_lo = sb("aT_hi", [P, KT, S], F32R), sb("aT_lo", [P, KT, S], F32R)
        nm = sb("neg_max", [P, NG, TT, G], F32)
        nmb = sb("neg_max_parts", [P, NG, TT, G, MAXROWS], BF16)
        mrow = sb("max_rows", [G * MAXROWS, 2, S], BF16)
        st1, mv1 = sb("st1", [P, TT, 6], F32), sb("mv1", [P, TT, 2], F32)
        st2, mv2 = sb("st2", [P, TT, 6], F32), sb("mv2", [P, TT, 2], F32)
        rs1, rs2 = sb("rs1", [P, 2, TT], F32), sb("rs2", [P, 2, TT], F32)
        minus_half = sb("minus_half", [P, TT], F32)
        ones_col = sb("ones_col", [P, 1], F32)
        low_most = sb("low_most", [P, 3], F32)
        low_all, low_flag = sb("low_all", [1, 1], F32), sb("low_flag", [1, 1], I32)
        ident, identb = sb("ident", [P, P], F32), sb("identb", [P, P], BF16)
        hide = sb("hide", [P, 2, P], BF16)

        smax = pb("smax", [P, MAX_BANKS, S], F32)
        sexp = pb("sexp", [P, EXP_BANKS, S], F32)
        pvo = pb("pvo", [P, S], F32)
        wk = pb("work", [P, 2, S], F32)
        smax_b = smax[:, :, :].bitcast(BF16)

        scr = nc.dram_tensor("parts", (4, H // 2, DK, 3, S), BF16, kind="Internal").ap()

        names = """wqkv_in wo_in wg_in wu_in wd_in c_in x_in res_in out_sent parts_sent0 parts_sent1 stack_in0 stack_in1
            m_in0 m_in1 m_in2 m_in3
            ones_col low_most low_sum low_all low_flag
            iden hidden ones_low ones_high half_set vones w_cast w_hi w_lo
            stat1 aggr1 var1 root1 norm1 stat2 aggr2 var2 root2 norm2
            x1T_full x1T_high x1T_low x2T_full x2T_high x2T_low
            qk_full qk_cos qk_swap qk_sin qk_rot qk_hi qk_rest qk_mid qk_low
            v_full v_out s_full s_out split_hi split t_full t_out masked
            pv_full o_copied o_turned o_inv o_norm aT_full aT_high aT_low wo_full wo_out
            gate_full sil_out up_full h_full h_high h_low y_full y_out""".split()
        E = {n: sem(n) for n in names}

        xv = x.rearrange("b (t p) d -> b p t d", p=P)
        ov = out.rearrange("b (t p) d -> b p t d", p=P)
        raw_f = rope[:, :, :, :].rearrange("p a b s -> p (a b s)")
        raw_i = prob[:, :, :].rearrange("p u s -> p (u s)")
        raw_qkv = raw_f[:, 0:KT * 3 * D].rearrange("p (k o) -> p k o", k=KT)
        raw_wo = attn[:, :, :, :].rearrange("p t h d -> p (t h d)")[:, 0:KT * D].rearrange("p (k o) -> p k o", k=KT)

        def raw_ffn(n, k):
            return raw_i[:, n * KT * HID:(n + 1) * KT * HID].rearrange("p (k o) -> p k o", k=k)

        block = ctx.enter_context(nc.Block())

        def at(steps, q):
            return [n for n, step in enumerate(steps) if step == q]

        def max_banks(q):
            return [(g, u) for g in range(NG) for u in range(UNITS) if max_step(g, u) == q]

        def spread(steps, q, prev, cur):
            return ([(-1, n) for n in at(steps, q + SLOTS) if prev] +
                    [(0, n) for n in at(steps, q) if cur])

        exp_steps = [EXP_STEP + n + (EXP_GAP if n >= GAP_FROM else 0) for n in range(NG * UNITS)]

        def exp_banks(q, prev, cur):
            return [(shift, n // UNITS, n % UNITS)
                    for shift, n in spread(exp_steps, q, prev, cur)]

        def fill(turn):
            turn(-1, False, False, True)
            turn(0, False, True, True)

        def turns(eng, turn):
            with eng.Fori(1, NB - 1) as b:
                turn(b, True, True, True)
            turn(NB - 1, True, True, False)
            turn(NB, True, False, False)

        @block.sync
        def _(sp):
            def max_rows(b, shift, g):
                wait_for(sp, E["s_out"], S_USES, b, shift, turn_use(g) + 1)
                for j in range(G):
                    sp.dma_start(qs[STACK:STACK + MAXROWS, G * g + j, :],
                                 mrow[MAXROWS * j:MAXROWS * (j + 1), g % 2, :]).then_inc(E[f"m_in{g}"], 16)

            def store_parts(b, t):
                sp.dma_start(scr[t].rearrange("h d n s -> (h d) n s"), part[:, t % 2, :, :])\
                    .then_inc(E[f"parts_sent{t % 2}"], 16)

            def load_stack(b, t):
                dst, singles = (qs, SINGLE_Q) if t % 2 == 0 else (ks, [2 - n for n in SINGLE_K])
                heads = slice(8 * (t // 2), 8 * (t // 2 + 1))
                sp.dma_start(dst[0:3 * DK, heads, :], scr[t].rearrange("h d n s -> (d n) h s"))\
                    .then_inc(E[f"stack_in{t // 2}"], 16)
                for i, n in enumerate(singles):
                    sp.dma_start(dst[DK * (3 + i):DK * (4 + i), heads, :], scr[t, :, :, n].rearrange("h d s -> d h s"))\
                        .then_inc(E[f"stack_in{t // 2}"], 16)

            def turn(b, prev, cur, nxt):
                steps = SP_AT if prev or cur else SP_START
                for q in range(SLOTS):
                    for shift, g in spread(SP_AT["rows"], q, prev, cur):
                        max_rows(b, shift, g)
                    if nxt and q == 0:
                        if cur and not prev:
                            wait_for(sp, E["x1T_full"], KT, b, 0, KT)
                        sp.dma_start(xt[:, :, :], xv[b + 1]).then_inc(E["x_in"], 16)
                    for _ in at(SP_AT["load_last"], q):
                        if cur:
                            if prev:
                                wait_for(sp, E["t_full"], T_USES, b, -1, T_USES)
                            else:
                                for t in (0, 1):
                                    wait_for(sp, E[f"parts_sent{t}"], 32, b, 0, 32)
                            load_stack(b, 2)
                            load_stack(b, 3)
                    for t in at(steps["store"], q):
                        if nxt:
                            wait_for(sp, E["qk_low"], 4, b, 1, t + 1)
                            store_parts(b, t)
                    for _ in at(steps["load_first"], q):
                        if nxt and cur:
                            wait_for(sp, E["t_full"], T_USES, b, 0, 2 * UNITS)
                            load_stack(b, 0)
                            load_stack(b, 1)
                        elif nxt:
                            for t in (0, 1):
                                wait_for(sp, E[f"parts_sent{t}"], 32, b, 1, 16)
                                load_stack(b, t)
                    for _ in at(SP_AT["out"], q):
                        if prev:
                            wait_for(sp, E["y_out"], KT, b, -1, 2)
                            sp.dma_start(ov[b - 1], res[:, :, :]).then_inc(E["out_sent"], 16)
                    for _ in at(SP_AT["res"], q):
                        if cur:
                            wait_for(sp, E["out_sent"], 16, b, -1, 16)
                            sp.dma_start(res[:, :, :], xv[b]).then_inc(E["res_in"], 16)

            fill(turn)
            turns(sp, turn)
            wait_for(sp, E["out_sent"], 16, NB, 0, 0)

        @block.gpsimd
        def _(pool):
            pool.memset(ident[:, :], 0.0).then_inc(E["iden"], 1)
            pool.memset(hide[:, :, :], 0.0).then_inc(E["hidden"], 1)
            pool.memset(ones_col[:, :], 1.0).then_inc(E["ones_col"], 1)
            pool.memset(minus_half[:, :], -0.5).then_inc(E["half_set"], 1)
            pool.memset(vaug[:, :, :, DK:32], 1.0).then_inc(E["vones"], 1)
            pool.wait_ge(E["iden"], 1)
            pool.affine_select(out=ident[:, :], in_=ident[:, :], compare_op=ALU.not_equal, fill=1.0,
                               base=0, pattern=[[-1, P]], channel_multiplier=1).then_inc(E["iden"], 1)
            pool.wait_ge(E["hidden"], 1)
            pool.affine_select(out=hide[:, :, :], in_=hide[:, :, :], compare_op=ALU.is_ge,
                               fill=BELOW_ALL, base=0, pattern=[[0, 2], [-1, P]],
                               channel_multiplier=1).then_inc(E["hidden"], 1)

            def root(b, shift, rs, var, done):
                wait_for(pool, var, 1, b, shift, 1)
                pool.tensor_tensor(rs[:, 1, :], rs[:, 0, :], minus_half[:, :], ALU.pow).then_inc(done, 1)

            def keep(b, shift, g, u):
                wait_for(pool, E["t_out"], T_USES, b, shift, UNITS * g + u + 1)
                if u % 5 == 2:
                    v = prob[:, u - 2:u + 1:2, 0:P]
                else:
                    v = prob[:, u, :].rearrange("p (k c) -> p k c", c=P)
                    v = v[:, 0:4:3, :] if u % 5 < 4 else v[:, 0:4:2, :]
                pool.affine_select(out=v, in_=v, compare_op=ALU.is_ge, fill=0.0, base=0,
                                   pattern=[[0, 2], [1, P]], channel_multiplier=-1).then_inc(E["masked"], 2)

            def rotate(b, t):
                wait_for(pool, E["qk_swap"], 8, b, 1, 2 * t + 2)
                pool.tensor_tensor(rope[:, t % 2, 1, :], rope[:, t % 2, 1, :], sin_sb[:, :], ALU.mult)\
                    .then_inc(E["qk_sin"], 1)
                wait_for(pool, E["qk_sin"], 4, b, 1, t + 1)
                pool.tensor_tensor(rope[:, t % 2, 0, :], rope[:, t % 2, 0, :], rope[:, t % 2, 1, :], ALU.add)\
                    .then_inc(E["qk_rot"], 1)

            def turn(b, prev, cur, nxt):
                steps = POOL_AT if prev or cur else POOL_START
                for q in range(SLOTS):
                    for shift, g, u in exp_banks(q, prev, cur):
                        if u % 5:
                            keep(b, shift, g, u)
                    for _ in at(steps["root1"], q):
                        if nxt:
                            root(b, 1, rs1, E["var1"], E["root1"])
                            if not cur:
                                half = ks[STACK:STACK + MAXROWS, 0:H // 2, :]
                                pool.wait_ge(E["root1"], 1)
                                pool.memset(half, 1.0).then_inc(E["ones_low"], 1)
                                pool.wait_ge(E["ones_low"], 1)
                    for _ in at(POOL_AT["root2"], q):
                        if prev:
                            root(b, -1, rs2, E["var2"], E["root2"])
                    for t in at(steps["rotate"], q):
                        if nxt:
                            rotate(b, t)
                    for t in at(steps["qk_rest"], q):
                        if nxt:
                            wait_for(pool, E["qk_hi"], 4, b, 1, t + 1)
                            pool.tensor_tensor(rope[:, t % 2, 0, :], rope[:, t % 2, 0, :], part[:, t % 2, (0, 2)[t % 2], :],
                                               ALU.subtract).then_inc(E["qk_rest"], 1)
                    for t in at(steps["qk_low"], q):
                        if nxt:
                            wait_for(pool, E["qk_mid"], 4, b, 1, t + 1)
                            pool.tensor_tensor(part[:, t % 2, (2, 0)[t % 2], :], rope[:, t % 2, 0, :],
                                               part[:, t % 2, 1, :],
                                               ALU.subtract).then_inc(E["qk_low"], 1)

                    for n in at(POOL_AT["h_low"], q):
                        if prev:
                            wait_for(pool, E["h_high"], FT, b, -1, n + 1)
                            pool.tensor_tensor(h_lo[:, n, :], sil[:, n % SIL_SLOTS, :], h_hi[:, n, :], ALU.subtract)\
                                .then_inc(E["h_low"], 1)

            fill(turn)
            turns(pool, turn)

        @block.scalar
        def _(act):
            act.dma_start(raw_qkv, wqkv.rearrange("(k p) o -> p k o", p=P)).then_inc(E["wqkv_in"], 16)
            act.dma_start(cos_sb[:, :], cos_t).then_inc(E["c_in"], 16)
            act.dma_start(sin_sb[:, :], sin_t).then_inc(E["c_in"], 16)
            act.dma_start(raw_wo, wo.rearrange("(k p) o -> p k o", p=P)).then_inc(E["wo_in"], 16)
            act.dma_start(raw_ffn(0, KT).bitcast(I32), wg.rearrange("(k p) o -> p k o", p=P)).then_inc(E["wg_in"], 16)
            act.dma_start(raw_ffn(1, KT).bitcast(I32), wu.rearrange("(k p) o -> p k o", p=P)).then_inc(E["wu_in"], 16)
            act.dma_start(raw_ffn(2, FT).bitcast(I32), wd.rearrange("(k p) o -> p k o", p=P)).then_inc(E["wd_in"], 16)

            def weight_high(dst, src):
                act.activation(dst, src, ACT.Copy).then_inc(E["w_hi"], 1)

            def weights(n):
                if n == 0:
                    act.wait_ge(E["wqkv_in"], 16)
                    weight_high(wqkv_hi[:, :, :], raw_qkv)
                elif n == 1:
                    act.wait_ge(E["wo_in"], 16)
                    weight_high(wo_hi[:, :, :], raw_wo)
                else:
                    act.wait_ge(E["w_cast"], n - 1)
                    dst, k = ((wg_hi, KT), (wu_hi, KT), (wd_hi, FT))[n - 2]
                    weight_high(dst[:, :, :], raw_ffn(n - 2, k))

            def high(b, shift, full, done, dst, k):
                wait_for(act, full, KT, b, shift, k + 1)
                act.activation(dst[:, k, :], wk[:, k, :], ACT.Copy).then_inc(done, 1)

            def values(b, i):
                wait_for(act, E["v_full"], 2, b, 0, i + 1)
                wait_for(act, E["pv_full"], NG, b, -1, NG)
                act.activation(vaug[:, 2 * i:2 * i + 2, :, 0:DK],
                               wk[:, i, :].rearrange("p (t h d) -> p t h d", t=2, d=DK), ACT.Copy)\
                    .then_inc(E["v_out"], 1)

            def exps(b, shift, g, u):
                k = UNITS * g + u
                wait_for(act, E["t_full"], T_USES, b, shift, k + 1)
                if u == 0:
                    wait_for(act, E["pv_full"], NG, b, shift, g)
                act.activation(prob[:, u, :], sexp[:, k % EXP_BANKS, :], ACT.Exp, scale=DK ** -0.5)\
                    .then_inc(E["t_out"], 1)

            def silu(b, n):
                wait_for(act, E["gate_full"], FT, b, -1, n + 1)
                if n >= SIL_SLOTS:
                    wait_for(act, E["h_low"], FT, b, -1, n - SIL_SLOTS + 1)
                act.activation(sil[:, n % SIL_SLOTS, :], wk[:, 0, :], ACT.Silu, scale=DEQ).then_inc(E["sil_out"], 1)

            def hidden_high(b, n):
                wait_for(act, E["h_full"], FT, b, -1, n + 1)
                act.activation(h_hi[:, n, :], sil[:, n % SIL_SLOTS, :], ACT.Copy).then_inc(E["h_high"], 1)

            def copy_o(b, shift, g):
                wait_for(act, E["pv_full"], NG, b, shift, g + 1)
                wait_for(act, E["o_turned"], NG, b, shift, g)
                act.activation(oT[:, :], pvo[:, :], ACT.Copy).then_inc(E["o_copied"], 1)

            def turn(b, prev, cur, nxt):
                steps = ACT_AT if prev or cur else ACT_START
                for q in range(SLOTS):
                    if not prev:
                        for n in at(ACT_START["weights"], q + SLOTS if cur else q):
                            weights(n)
                    for shift, g in spread(ACT_AT["copy_o"], q, prev, cur):
                        copy_o(b, shift, g)
                    for i in at(ACT_AT["v"], q):
                        if cur:
                            values(b, i)
                    for k in at(ACT_AT["aT"], q):
                        if prev:
                            high(b, -1, E["aT_full"], E["aT_high"], aT_hi, k)
                    for k in at(steps["x1T"], q):
                        if nxt:
                            high(b, 1, E["x1T_full"], E["x1T_high"], x1T_hi, k)
                    for k in at(ACT_AT["x2T"], q):
                        if prev:
                            high(b, -1, E["x2T_full"], E["x2T_high"], x2T_hi, k)
                    for n in range(FT):
                        if prev and ACT_AT["silu"][n] == q:
                            silu(b, n)
                        if prev and n and ACT_AT["h_high"][n - 1] == q:
                            hidden_high(b, n - 1)
                    if prev and ACT_AT["h_high"][FT - 1] == q:
                        hidden_high(b, FT - 1)
                    for shift, g, u in exp_banks(q, prev, cur):
                        exps(b, shift, g, u)
                    for t in at(steps["qk_hi"], q):
                        if nxt:
                            wait_for(act, E["qk_rot"], 4, b, 1, t + 1)
                            wait_for(act, E[f"parts_sent{t % 2}"], 32, b, 1, 16 * (t // 2))
                            act.activation(part[:, t % 2, (0, 2)[t % 2], :], rope[:, t % 2, 0, :], ACT.Copy)\
                                .then_inc(E["qk_hi"], 1)
                    for t in at(steps["qk_mid"], q):
                        if nxt:
                            wait_for(act, E["qk_rest"], 4, b, 1, t + 1)
                            act.activation(part[:, t % 2, 1, :], rope[:, t % 2, 0, :], ACT.Copy)\
                                .then_inc(E["qk_mid"], 1)

            fill(turn)
            turns(act, turn)

        @block.vector
        def _(dve):
            def weight_low(dst, src, hi, n):
                dve.wait_ge(E["w_hi"], n + 1)
                dve.tensor_tensor(dst, src, hi, ALU.subtract).then_inc(E["w_lo"], 1)

            def weight_cast(n):
                dve.wait_ge(E[("wg_in", "wu_in", "wd_in")[n]], 16)
                raw = raw_ffn(n, FT if n == 2 else KT)
                dve.tensor_copy(raw, raw.bitcast(I32)).then_inc(E["w_cast"], 1)

            def weights(n):
                if n == 0:
                    weight_low(wqkv_lo[:, :, :], raw_qkv, wqkv_hi[:, :, :], 0)
                elif n == 1:
                    weight_low(wo_lo[:, :, :], raw_wo, wo_hi[:, :, :], 1)
                else:
                    dst, hi, k = ((wg_lo, wg_hi, KT), (wu_lo, wu_hi, KT), (wd_lo, wd_hi, FT))[n - 2]
                    weight_low(dst[:, :, :], raw_ffn(n - 2, k), hi[:, :, :], n)

            dve.wait_ge(E["iden"], 2)
            dve.tensor_copy(identb[:, :], ident[:, :]).then_inc(E["iden"], 1)

            def norm_stats(b, shift, src, st, mv, rs, which):
                for i in range(TT):
                    last = dve.bn_stats(st[:, i, :], src[:, i, :])
                last.then_inc(E["stat" + which], 1)
                wait_for(dve, E["stat" + which], 1, b, shift, 1)
                for i in range(TT):
                    dve.bn_aggr(mv[:, i, :], st[:, i, :]).then_inc(E["aggr" + which], 2)
                wait_for(dve, E["aggr" + which], 2 * TT, b, shift, 2 * TT)
                dve.tensor_scalar(rs[:, 0, :], mv[:, :, 1], EPS, None, ALU.add).then_inc(E["var" + which], 1)

            def norm_apply(b, shift, dst, src, mv, rs, which):
                wait_for(dve, E["root" + which], 1, b, shift, 1)
                for i in range(TT):
                    last = dve.tensor_scalar(dst[:, i, :], src[:, i, :], mv[:, i, 0:1], rs[:, 1, i:i + 1],
                                             ALU.subtract, ALU.mult)
                last.then_inc(E["norm" + which], 1)

            def low(b, shift, high, done, dst, hi, k):
                wait_for(dve, high, KT, b, shift, k + 1)
                dve.tensor_tensor(dst[:, k, :], wk[:, k, :], hi[:, k, :], ALU.subtract).then_inc(done, 1)

            def row_max(b, g, u):
                use, r, v = max_use(g, u), u // 5, u % 5
                bank = smax[:, use % MAX_BANKS, :]
                wait_for(dve, E["s_full"], S_USES, b, 0, use + 1)
                if v == 4:
                    last = dve.tensor_reduce(nm[:, g, 1, 2 * r:2 * r + 2],
                                             bank.rearrange("p (h c) -> p h c", h=2), AX.X, ALU.max, negate=True)
                else:
                    h = 2 * r + v // 2
                    if v % 2 == 0:
                        last = dve.tensor_reduce(nm[:, g, 3, h:h + 1], bank, AX.X, ALU.max, negate=True)
                    else:
                        dve.tensor_reduce(nm[:, g, 2, h:h + 1], bank[:, 0:3 * P], AX.X, ALU.max, negate=True)
                        last = dve.tensor_reduce(nm[:, g, 0, h:h + 1], bank[:, 3 * P:S], AX.X, ALU.max, negate=True)
                last.then_inc(E["s_out"], 1)

            def split_max(b, g):
                wait_for(dve, E["s_out"], S_USES, b, 0, max_use(g, UNITS - 1) + 1)
                dve.tensor_copy(nmb[:, g, :, :, 0], nm[:, g, :, :]).then_inc(E["split_hi"], 1)
                wait_for(dve, E["split_hi"], NG, b, 0, g + 1)
                dve.tensor_tensor(nmb[:, g, :, :, 1], nm[:, g, :, :], nmb[:, g, :, :, 0], ALU.subtract)\
                    .then_inc(E["split"], 1)

            def copy_max(b, g):
                use = turn_use(g)
                wait_for(dve, E["s_full"], S_USES, b, 0, use + 1)
                if g < 2:
                    wait_for(dve, E[f"m_in{g + 2}"], 64, b, -1, 64)
                else:
                    wait_for(dve, E[f"m_in{g - 2}"], 64, b, 0, 64)
                dve.tensor_copy(mrow[:, g % 2, :], smax_b[0:G * MAXROWS, use % MAX_BANKS, 0:S])\
                    .then_inc(E["s_out"], 1)

            def attn_norm(b, shift, g):
                o = pvo[:, :].rearrange("p (t h c) -> p t h c", t=TT, h=G)
                wait_for(dve, E["o_turned"], NG, b, shift, g + 1)
                dve.reciprocal(rsum[:, :, :, :], o[:, :, :, DK:DK + 1]).then_inc(E["o_inv"], 1)
                wait_for(dve, E["o_inv"], NG, b, shift, g + 1)
                if g == 0:
                    wait_for(dve, E["aT_full"], KT, b, shift - 1, KT)
                dve.tensor_tensor(attn[:, :, G * g:G * (g + 1), :], o[:, :, :, 0:DK],
                                  rsum[:, :, :, :].broadcast_to([P, TT, G, DK]), ALU.mult)\
                    .then_inc(E["o_norm"], 1)

            def hidden_full(b, n):
                wait_for(dve, E["up_full"], FT, b, -1, n + 1)
                wait_for(dve, E["sil_out"], FT, b, -1, n + 1)
                dve.scalar_tensor_tensor(out=sil[:, n % SIL_SLOTS, :], in0=wk[:, 1, :], scalar=DEQ,
                                         in1=sil[:, n % SIL_SLOTS, :], op0=ALU.mult, op1=ALU.mult)\
                    .then_inc(E["h_full"], 1)

            def look_at_lows():
                for n, low_part in enumerate((wg_lo, wu_lo, wd_lo)):
                    last = dve.tensor_reduce(low_most[:, n:n + 1], low_part[:, :, :].bitcast(F32), AX.XY,
                                             ALU.max, apply_absolute_value=True)
                last.then_inc(E["low_most"], 1)
                dve.wait_ge(E["low_sum"], 1)
                dve.tensor_reduce(low_all[:, :], wk[0:1, 0, 0:3], AX.X, ALU.add).then_inc(E["low_all"], 1)
                dve.wait_ge(E["low_all"], 1)
                dve.tensor_scalar(low_flag[:, :], low_all[:, :], 1.0, None, ALU.min).then_inc(E["low_flag"], 1)

            def turn(b, prev, cur, nxt):
                steps = DVE_AT if prev or cur else DVE_START
                for q in range(SLOTS):
                    if not prev:
                        for n in at(DVE_START["cast"], q + SLOTS if cur else q):
                            weight_cast(n)
                        for n in at(DVE_START["weights"], q + SLOTS if cur else q):
                            weights(n)
                    for g, u in max_banks(q):
                        if cur:
                            if g and u == TURN_AFTER + 1:
                                if g == NG - 1 and nxt:
                                    for t in (0, 1):
                                        wait_for(dve, E[f"parts_sent{t}"], 32, b, 1, 32)
                                copy_max(b, g - 1)
                            row_max(b, g, u)
                    for g in at(DVE_AT["split"], q):
                        if cur:
                            split_max(b, g)
                    for _ in at(DVE_AT["copy_max"], q):
                        if cur:
                            copy_max(b, NG - 1)
                    for shift, g in spread(DVE_AT["norm_o"], q, prev, cur):
                        attn_norm(b, shift, g)
                    for _ in at(steps["stat1"], q):
                        if nxt:
                            wait_for(dve, E["x_in"], 16, b, 1, 16)
                            norm_stats(b, 1, xt, st1, mv1, rs1, "1")
                    for _ in at(steps["apply1"], q):
                        if nxt:
                            norm_apply(b, 1, xt, xt, mv1, rs1, "1")
                    for k in at(DVE_AT["aT"], q):
                        if prev:
                            low(b, -1, E["aT_high"], E["aT_low"], aT_lo, aT_hi, k)
                    for i in at(DVE_AT["wo"], q):
                        if prev:
                            wait_for(dve, E["res_in"], 16, b, -1, 16)
                            wait_for(dve, E["wo_full"], 2, b, -1, i + 1)
                            dve.tensor_tensor(res[:, 2 * i:2 * i + 2, :],
                                              wk[:, i, :].rearrange("p (t d) -> p t d", t=2),
                                              res[:, 2 * i:2 * i + 2, :], ALU.add).then_inc(E["wo_out"], 1)
                    for k in at(steps["x1T"], q):
                        if nxt:
                            low(b, 1, E["x1T_high"], E["x1T_low"], x1T_lo, x1T_hi, k)
                    for _ in at(DVE_AT["stat2"], q):
                        if prev:
                            wait_for(dve, E["wo_out"], 2, b, -1, 2)
                            norm_stats(b, -1, res, st2, mv2, rs2, "2")
                    for _ in at(DVE_AT["apply2"], q):
                        if prev:
                            norm_apply(b, -1, xt, res, mv2, rs2, "2")
                    for t in at(steps["qk"], q):
                        if nxt:
                            wait_for(dve, E["qk_full"], 4, b, 1, t + 1)
                            if not cur and t == 0:
                                dve.wait_ge(E["c_in"], 32)
                            if t % 2 == 0:
                                wait_for(dve, E[f"stack_in{t // 2}"], 2 * 16 * 4, b, 1, 0)
                            if t >= 2:
                                wait_for(dve, E["qk_low"], 4, b, 1, t - 1)
                            dve.tensor_tensor(rope[:, t % 2, 0, :], wk[:, t % 2, :], cos_sb[:, :], ALU.mult)\
                                .then_inc(E["qk_cos"], 1)
                            dve.stream_shuffle(rope[:, t % 2, 1, :], wk[:, t % 2, :], SWAP_PAIRS)\
                                .then_inc(E["qk_swap"], 2)
                            if not cur and t == 1:
                                half = ks[STACK:STACK + MAXROWS, H // 2:H, :]
                                dve.memset(half, 1.0).then_inc(E["ones_high"], 1)
                    for k in at(DVE_AT["x2T"], q):
                        if prev:
                            low(b, -1, E["x2T_high"], E["x2T_low"], x2T_lo, x2T_hi, k)
                    for n in at(DVE_AT["h_full"], q):
                        if prev:
                            hidden_full(b, n)
                    for i in at(DVE_AT["y"], q):
                        if prev:
                            wait_for(dve, E["y_full"], 2, b, -1, i + 1)
                            dve.scalar_tensor_tensor(out=res[:, 2 * i:2 * i + 2, :],
                                                     in0=wk[:, i, :].rearrange("p (t d) -> p t d", t=2), scalar=DEQ,
                                                     in1=res[:, 2 * i:2 * i + 2, :], op0=ALU.mult, op1=ALU.add)\
                                .then_inc(E["y_out"], 1)

            fill(turn)
            look_at_lows()
            turns(dve, turn)

        @block.tensor
        def _(pe):
            def three(dst, k_tiles, w_hi, w_lo, m_hi, m_lo, exact=None):
                for k in range(k_tiles):
                    products = [(w_hi, m_hi)]
                    if exact != "moving":
                        products.append((w_hi, m_lo))
                    if exact != "stationary":
                        products.append((w_lo, m_hi))
                    for n, (w, m) in enumerate(products):
                        last = pe.matmul(dst, w(k), m(k), start=k == n == 0,
                                         stop=k == k_tiles - 1 and n == len(products) - 1)
                return last

            def project(n, w):
                return lambda k: w[:, k, P * n:P * (n + 1)]

            def tokens(i, a):
                return lambda k: a[:, k, P * i:P * (i + 1)]

            def turn_x(src, full, k):
                for i in range(TT):
                    last = pe.transpose(wk[:, k, P * i:P * (i + 1)], src[:, i, P * k:P * (k + 1)], ident[:, :])
                last.then_inc(full, 1)

            def turn_o(b, shift, g):
                wait_for(pe, E["o_copied"], NG, b, shift, g + 1)
                for i in range(TT):
                    last = pe.transpose(pvo[:, P * i:P * (i + 1)], oT[:, P * i:P * (i + 1)], ident[:, :])
                last.then_inc(E["o_turned"], 1)

            def scores_max(b, g, u):
                use, r, v = max_use(g, u), u // 5, u % 5
                bank = smax[:, use % MAX_BANKS, :]
                if u == 0 and g % 2 == 0:
                    wait_for(pe, E[f"stack_in{g // 2}"], 2 * 16 * 4, b, 1, 0)
                ring_free(pe, E["s_out"], S_USES, MAX_BANKS, b, 0, use)
                head = G * g + 2 * r + v // 2

                def score(h, i, at):
                    return pe.matmul(bank[:, at:at + P * (i + 1)], qs[0:STACK, h, P * i:P * (i + 1)],
                                     ks[0:STACK, h, 0:P * (i + 1)], start=False, stop=True,
                                     skip_group_check=True)

                if v == 4:
                    diag = bank.rearrange("p (k c) -> p k c", c=P)[:, 1:4:2, :]
                    pe.matmul(diag, identb[:, :], hide[:, :, :], start=True, stop=False, skip_group_check=True)
                    score(G * g + 2 * r, 1, 0)
                    last = score(G * g + 2 * r + 1, 1, 2 * P)
                elif v % 2 == 0:
                    pe.matmul(bank[:, 3 * P:S], identb[:, :], hide[:, 0, :], start=True, stop=False,
                              skip_group_check=True)
                    last = score(head, 3, 0)
                else:
                    pe.matmul(bank[:, 2 * P:S], identb[:, :], hide[:, :, :].rearrange("p k c -> p (k c)"),
                              start=True, stop=False, skip_group_check=True)
                    score(head, 2, 0)
                    last = score(head, 0, 3 * P)
                last.then_inc(E["s_full"], 1)

            def turn_max(b, g):
                use = turn_use(g)
                wait_for(pe, E["split"], NG, b, 0, g + 1)
                ring_free(pe, E["s_out"], S_USES, MAX_BANKS, b, 0, use)
                for i in range(TT):
                    last = pe.transpose(smax_b[0:G * MAXROWS, use % MAX_BANKS, P * i:P * (i + 1)],
                                        nmb[:, g, i, :, :].rearrange("p h n -> p (h n)"), identb[:, :])
                last.then_inc(E["s_full"], 1)

            def scores_exp(b, shift, g, u):
                k, r, v = UNITS * g + u, u // 5, u % 5
                bank = sexp[:, k % EXP_BANKS, :]
                if u == 0:
                    wait_for(pe, E[f"m_in{g}"], 64, b, shift, 64)
                ring_free(pe, E["t_out"], T_USES, EXP_BANKS, b, shift, k)
                rows = STACK + MAXROWS
                head = G * g + 2 * r + v // 2

                def score(h, j, at):
                    return pe.matmul(bank[:, at:at + S - P * j], ks[0:rows, h, P * j:P * (j + 1)],
                                     qs[0:rows, h, P * j:S], start=True, stop=True)

                if v == 4:
                    score(G * g + 2 * r, 2, 0)
                    last = score(G * g + 2 * r + 1, 2, 2 * P)
                elif v % 2 == 0:
                    last = score(head, 0, 0)
                else:
                    score(head, 1, 0)
                    last = score(head, 3, 3 * P)
                last.then_inc(E["t_full"], 1)

            def prob_values(b, shift, g):
                wait_for(pe, E["t_out"], T_USES, b, shift, UNITS * (g + 1))
                wait_for(pe, E["masked"], 16 * NG, b, shift, 16 * (g + 1))
                wait_for(pe, E["v_out"], 2, b, shift, 2)
                wait_for(pe, E["o_norm"], NG, b, shift, g)
                for j in range(TT):
                    for c in range(G):
                        u = 5 * (c // 2) + 2 * (c % 2)
                        p = (prob[:, u, :], prob[:, u + 1, 0:3 * P],
                             prob[:, 5 * (c // 2) + 4, 2 * P * (c % 2):2 * P * (c % 2 + 1)],
                             prob[:, u + 1, 3 * P:S])[j]
                        last = pe.matmul(pvo[32 * c:32 * (c + 1), P * j:S], vaug[:, j, G * g + c, :], p,
                                         start=j == 0, stop=j == TT - 1)
                last.then_inc(E["pv_full"], 1)

            def gate_up(b, n, exact):
                if n == 0:
                    wait_for(pe, E["x2T_low"], KT, b, -1, KT)
                else:
                    wait_for(pe, E["sil_out"], FT, b, -1, n)
                three(wk[:, 0, :], KT, project(n, wg_hi), project(n, wg_lo),
                      lambda k: x2T_hi[:, k, :], lambda k: x2T_lo[:, k, :],
                      "stationary" if exact else None).then_inc(E["gate_full"], 1)
                if n:
                    wait_for(pe, E["h_full"], FT, b, -1, n)
                three(wk[:, 1, :], KT, project(n, wu_hi), project(n, wu_lo),
                      lambda k: x2T_hi[:, k, :], lambda k: x2T_lo[:, k, :],
                      "stationary" if exact else None).then_inc(E["up_full"], 1)

            def turn(b, prev, cur, nxt, exact=False):
                steps = PE_AT if prev or cur else PE_START
                for q in range(SLOTS):
                    for g, u in max_banks(q):
                        if cur:
                            scores_max(b, g, u)
                            if g and u == TURN_AFTER:
                                turn_max(b, g - 1)
                    for _ in at(PE_AT["turn_max"], q):
                        if cur:
                            turn_max(b, NG - 1)
                    if cur and not prev and q == EXP_STEP:
                        pe.wait_ge(E["w_lo"], 5)
                        pe.wait_ge(E["ones_low"], 1)
                        pe.wait_ge(E["ones_high"], 1)
                        pe.wait_ge(E["vones"], 1)
                    for shift, g, u in exp_banks(q, prev, cur):
                        scores_exp(b, shift, g, u)
                    for shift, g in spread(PE_AT["pv"], q, prev, cur):
                        prob_values(b, shift, g)
                    for shift, g in spread(PE_AT["turn_o"], q, prev, cur):
                        turn_o(b, shift, g)
                    for i in at(PE_AT["v"], q):
                        if cur:
                            if prev:
                                wait_for(pe, E["o_norm"], NG, b, -1, NG - 1)
                            else:
                                wait_for(pe, E["qk_swap"], 8, b, 0, 2 * (i + 3))
                            for t in (2 * i, 2 * i + 1):
                                last = three(wk[:, i, D * (t % 2):D * (t % 2 + 1)], KT,
                                             tokens(t, x1T_hi), tokens(t, x1T_lo),
                                             lambda k: wqkv_hi[:, k, 2 * D:3 * D], lambda k: wqkv_lo[:, k, 2 * D:3 * D])
                            last.then_inc(E["v_full"], 1)
                    for k in at(PE_AT["aT"], q):
                        if prev:
                            wait_for(pe, E["o_norm"], NG, b, -1, NG)
                            if cur:
                                wait_for(pe, E["v_out"], 2, b, 0, k + 1)
                            turn_x(attn[:, :, :, :].rearrange("p t h d -> p t (h d)"), E["aT_full"], k)
                    for i in at(PE_AT["wo"], q):
                        if prev:
                            wait_for(pe, E["aT_low"], KT, b, -1, KT)
                            for t in (2 * i, 2 * i + 1):
                                last = three(wk[:, i, D * (t % 2):D * (t % 2 + 1)], KT,
                                             tokens(t, aT_hi), tokens(t, aT_lo),
                                             lambda k: wo_hi[:, k, :], lambda k: wo_lo[:, k, :])
                            last.then_inc(E["wo_full"], 1)
                    for k in at(steps["x1T"], q):
                        if nxt:
                            wait_for(pe, E["norm1"], 1, b, 1, 1)
                            if prev:
                                wait_for(pe, E["wo_out"], 2, b, -1, k + 1)
                            elif cur:
                                wait_for(pe, E["v_out"], 2, b, 0, k + 1)
                            turn_x(xt, E["x1T_full"], k)
                    for t in at(steps["qk"], q):
                        if nxt:
                            if t == 0:
                                wait_for(pe, E["x1T_low"], KT, b, 1, KT)
                            if t >= 2:
                                wait_for(pe, E["qk_swap"], 8, b, 1, 2 * (t - 1))
                            n = KT * (t % 2) + t // 2
                            three(wk[:, t % 2, :], KT, project(n, wqkv_hi), project(n, wqkv_lo),
                                  lambda k: x1T_hi[:, k, :], lambda k: x1T_lo[:, k, :]).then_inc(E["qk_full"], 1)
                    for k in at(PE_AT["x2T"], q):
                        if prev:
                            wait_for(pe, E["norm2"], 1, b, -1, 1)
                            if nxt:
                                wait_for(pe, E["qk_swap"], 8, b, 1, 2 * (k + 3))
                            turn_x(xt, E["x2T_full"], k)
                    for n in at(PE_AT["gate"], q):
                        if prev:
                            gate_up(b, n, exact)
                    for i in at(PE_AT["down"], q):
                        if prev:
                            wait_for(pe, E["h_low"], FT, b, -1, FT)
                            for t in (2 * i, 2 * i + 1):
                                last = three(wk[:, i, D * (t % 2):D * (t % 2 + 1)], FT,
                                             tokens(t, h_hi), tokens(t, h_lo),
                                             lambda k: wd_hi[:, k, :], lambda k: wd_lo[:, k, :],
                                             "moving" if exact else None)
                            last.then_inc(E["y_full"], 1)

            pe.wait_ge(E["iden"], 3)
            pe.wait_ge(E["w_lo"], 1)
            pe.wait_ge(E["hidden"], 2)
            fill(turn)
            pe.wait_ge(E["low_most"], 1)
            pe.wait_ge(E["ones_col"], 1)
            pe.wait_ge(E["qk_swap"], 16)
            pe.matmul(wk[0:1, 0, 0:3], ones_col[:, :], low_most[:, :], start=True, stop=True)\
                .then_inc(E["low_sum"], 1)
            pe.wait_ge(E["low_flag"], 1)
            flag = pe.value_load(low_flag[0:1, 0:1], min_val=0, max_val=1)
            with pe.If(flag == 0):
                turns(pe, lambda b, prev, cur, nxt: turn(b, prev, cur, nxt, exact=True))
            with pe.Else():
                turns(pe, turn)


def kernel(L0_attn_x, L0_attn_Wq, L0_attn_Wk, L0_attn_Wv, L0_attn_Wo, L0_ffn_w_gate, L0_ffn_w_up, L0_ffn_w_down):
    import numpy as _np
    import concourse.bacc as _bacc
    from concourse import mybir as _mybir
    from concourse.bass_utils import run_bass_kernel_spmd as _run

    pos = _np.arange(S, dtype=_np.float32)
    inv_freq = (1.0 / _np.float32(10000.0) ** (_np.arange(0, DK, 2, dtype=_np.float32) / DK)).astype(_np.float32)
    angles = inv_freq[(_np.arange(P) % DK) // 2][:, None] * pos[None, :]
    sign = _np.where(_np.arange(P) % 2 == 0, -1.0, 1.0).astype(_np.float32)[:, None]
    arrays = {
        "x": _np.ascontiguousarray(L0_attn_x),
        "wqkv": _np.ascontiguousarray(_np.concatenate(
            [_np.transpose(_np.asarray(w)) for w in (L0_attn_Wq, L0_attn_Wk, L0_attn_Wv)], axis=1)),
        "wo": _np.ascontiguousarray(_np.transpose(_np.asarray(L0_attn_Wo))),
        "wg": _np.ascontiguousarray(_np.transpose(_np.asarray(L0_ffn_w_gate))),
        "wu": _np.ascontiguousarray(_np.transpose(_np.asarray(L0_ffn_w_up))),
        "wd": _np.ascontiguousarray(_np.transpose(_np.asarray(L0_ffn_w_down))),
        "cos_t": _np.cos(angles).astype(_np.float32),
        "sin_t": (sign * _np.sin(angles)).astype(_np.float32),
    }
    nc = _bacc.Bacc("TRN2", target_bir_lowering=False, num_devices=1)
    args = [nc.dram_tensor(n, a.shape, _mybir.dt.from_np(a.dtype), kind="ExternalInput").ap()
            for n, a in arrays.items()]
    args.append(nc.dram_tensor("out", (NB, S, D), _mybir.dt.float32, kind="ExternalOutput").ap())
    preln_block(nc, *args)
    r = _run(nc, [arrays], core_ids=[0])
    return r.results[0]["out"]
```
